# Optimizing a Trainium2 kernel written in Bass

```python
import numpy as np
import jax
import jax.numpy as jnp

def _softmax(x, axis=-1):
    return jax.nn.softmax(x, axis=axis)

def _gelu(x):
    return jax.nn.gelu(x, approximate=True)

def _silu(x):
    return jax.nn.silu(x)

def _sigmoid(x):
    return jax.nn.sigmoid(x)

def _layernorm(x, axis=-1, eps=1e-05):
    m = jnp.mean(x, axis=axis, keepdims=True)
    v = jnp.var(x, axis=axis, keepdims=True)
    return (x - m) / jnp.sqrt(v + eps)

def _scatter_add(tgt, idx, src, axis=0):
    return tgt.at[idx].add(src)

def _segment_sum(src, seg, n):
    return jax.ops.segment_sum(src, seg, n)
kernel_name = 'mk_adj_preln_d2_adj_r2_35f4e7'

def setup_inputs(seed: int=0):
    np.random.seed(seed)
    _w = jnp.asarray

    def _rec_inputs():
        import jax
        import jax.numpy as jnp
        _gk = jax.random.key(seed)
        x = -0.0005207 + 1.001 * jax.random.normal(jax.random.fold_in(_gk, 1), (16, 512, 128), jnp.float32)
        _a = jax.random.bernoulli(jax.random.fold_in(_gk, 2), 0.03125, (16, 512, 512))
        _a = jnp.logical_or(_a, jnp.eye(512, dtype=bool))
        adj = _a.astype(jnp.int32)
        return (x, adj)
    x, adj = _rec_inputs()

    def _L0_gnn_setup():
        import jax, jax.numpy as jnp
        import numpy as np
        BS, N, D, R = (16, 256, 128, 2)
        key = jax.random.key(seed)
        ks = jax.random.split(key, 9)
        s = 1.0 / np.sqrt(D)
        return {'encoded_spans': jax.random.normal(ks[0], (BS, N, D), dtype=jnp.float32), 'w_rel1': jax.random.normal(ks[1], (R, D, D), dtype=jnp.float32) * s, 'w_root1': jax.random.normal(ks[2], (D, D), dtype=jnp.float32) * s, 'b1': jnp.zeros((D,), dtype=jnp.float32), 'w_rel2': jax.random.normal(ks[3], (R, D, D), dtype=jnp.float32) * s, 'w_root2': jax.random.normal(ks[4], (D, D), dtype=jnp.float32) * s, 'b2': jnp.zeros((D,), dtype=jnp.float32), 'aug_adj': jax.random.randint(ks[5], (BS, N, N), 0, 16, dtype=jnp.int64), 'punct_graph': jax.random.randint(ks[6], (BS, N, N), 0, 16, dtype=jnp.int64)}
    _L0_gnn_all = _L0_gnn_setup()
    _L0_gnn_in = {k: v for k, v in _L0_gnn_all.items() if k in ('w_rel1', 'w_root1', 'b1', 'w_rel2', 'w_root2', 'b2')}
    del _L0_gnn_all

    def _L1_gnn_setup():
        import jax, jax.numpy as jnp
        import numpy as np
        LEAKY_SLOPE = 0.2
        NEG_INF = -9000000000000000.0

        def _edge_scores(h, a_k):
            e = jnp.einsum('bid,bjd->bij', h * a_k[:, 0], h)
            return jax.nn.leaky_relu(e, negative_slope=LEAKY_SLOPE)
        key = jax.random.key(seed)
        k1, k2, k3, k4, k5, k6 = jax.random.split(key, 6)
        B, N, D = (32, 256, 128)
        hidden = jax.random.normal(k1, (B, N, D), dtype=jnp.float32)
        adj = jax.random.randint(k2, (B, N, N), 0, 5, dtype=jnp.int32)
        a_0 = jax.random.normal(k3, (D, 1), dtype=jnp.float32)
        a_1 = jax.random.normal(k4, (D, 1), dtype=jnp.float32)
        a_2 = jax.random.normal(k5, (D, 1), dtype=jnp.float32)
        a_3 = jax.random.normal(k6, (D, 1), dtype=jnp.float32)
        return {'hidden': hidden, 'adj': adj, 'a_0': a_0, 'a_1': a_1, 'a_2': a_2, 'a_3': a_3}
    _L1_gnn_all = _L1_gnn_setup()
    _L1_gnn_in = {k: v for k, v in _L1_gnn_all.items() if k in ('a_0', 'a_1', 'a_2', 'a_3')}
    del _L1_gnn_all
    return {'x': x, 'adj': adj, 'L0_gnn_w_rel1': _L0_gnn_in['w_rel1'], 'L0_gnn_w_root1': _L0_gnn_in['w_root1'], 'L0_gnn_b1': _L0_gnn_in['b1'], 'L0_gnn_w_rel2': _L0_gnn_in['w_rel2'], 'L0_gnn_w_root2': _L0_gnn_in['w_root2'], 'L0_gnn_b2': _L0_gnn_in['b2'], 'L1_gnn_a_0': _L1_gnn_in['a_0'], 'L1_gnn_a_1': _L1_gnn_in['a_1'], 'L1_gnn_a_2': _L1_gnn_in['a_2'], 'L1_gnn_a_3': _L1_gnn_in['a_3']}

def reference(x, adj, L0_gnn_w_rel1, L0_gnn_w_root1, L0_gnn_b1, L0_gnn_w_rel2, L0_gnn_w_root2, L0_gnn_b2, L1_gnn_a_0, L1_gnn_a_1, L1_gnn_a_2, L1_gnn_a_3):
    import jax
    import jax.numpy as jnp

    def _L0_gnn_ref(encoded_spans, w_rel1, w_root1, b1, w_rel2, w_root2, b2, aug_adj, punct_graph):
        import jax, jax.numpy as jnp
        import numpy as np
        BS, N, D, R = (16, 256, 128, 2)
        mask_punct = (punct_graph == 1) & (aug_adj != 1)
        mask_aug = aug_adj == 1
        masks = jnp.stack([mask_punct, mask_aug]).astype(encoded_spans.dtype)
        deg = jnp.maximum(masks.sum(axis=2), 1.0)[..., None]

        def conv(x, w_rel, w_root, b):
            out = jnp.einsum('bnd,de->bne', x, w_root) + b
            for r in range(R):
                agg = jnp.einsum('bij,bid->bjd', masks[r], x) / deg[r]
                out = out + jnp.einsum('bjd,de->bje', agg, w_rel[r])
            return out
        h = jax.nn.elu(conv(encoded_spans, w_rel1, w_root1, b1))
        h = jax.nn.elu(conv(h, w_rel2, w_root2, b2))
        return h

    def _L1_gnn_ref(hidden, adj, a_0, a_1, a_2, a_3):
        import jax, jax.numpy as jnp
        import numpy as np
        LEAKY_SLOPE = 0.2
        NEG_INF = -9000000000000000.0

        def _edge_scores(h, a_k):
            e = jnp.einsum('bid,bjd->bij', h * a_k[:, 0], h)
            return jax.nn.leaky_relu(e, negative_slope=LEAKY_SLOPE)
        h = hidden
        e_0 = _edge_scores(h, a_0)
        e_1 = _edge_scores(h, a_1)
        e_2 = _edge_scores(h, a_2)
        e_3 = _edge_scores(h, a_3)
        scores = jnp.where(adj == 1, e_0, NEG_INF)
        scores = jnp.where(adj == 2, e_1, scores)
        scores = jnp.where(adj == 3, e_2, scores)
        scores = jnp.where(adj == 4, e_3, scores)
        alpha = jax.nn.softmax(scores, axis=-1)
        return jnp.einsum('bij,bjd->bid', alpha, h)
    h = jnp.maximum(_layernorm(x, axis=-1), 0.0)
    x = x + _L0_gnn_ref(h, L0_gnn_w_rel1, L0_gnn_w_root1, L0_gnn_b1, L0_gnn_w_rel2, L0_gnn_w_root2, L0_gnn_b2, adj, adj)
    h = jnp.maximum(_layernorm(x, axis=-1), 0.0)
    x = x + _L1_gnn_ref(h, adj, L1_gnn_a_0, L1_gnn_a_1, L1_gnn_a_2, L1_gnn_a_3)
    return x

_drawn_inputs = setup_inputs


def setup_inputs(seed=0):
    import zlib

    import numpy as np

    out = dict(_drawn_inputs(seed))
    spreads = {'L0_gnn_b1': (0.0, 0.1), 'L0_gnn_b2': (0.0, 0.1)}
    factors = {}
    for name, (base, spread) in spreads.items():
        noise = np.random.default_rng([zlib.crc32(name.encode()), seed]).standard_normal(out[name].shape)
        drawn = base * np.exp(spread * noise) if base else spread * noise
        out[name] = jnp.asarray(drawn.astype(out[name].dtype))
    for name, factor in factors.items():
        out[name] = (out[name] * factor).astype(out[name].dtype)
    return out
```

```python
from contextlib import ExitStack

import concourse.bass as bass
from concourse import mybir

P = 128
BATCHES, NODES, DIM = 16, 512, 128
TILES = NODES // P
RELATION = 1
LN_EPS = 1e-5
SLOPE = 0.2
NEG_INF = -9e15
AWAY = -NEG_INF / SLOPE
KINDS = 4
UNROLL = 4
WEIGHTS = 5 + KINDS
VCOLS = DIM + 2

F32 = mybir.dt.float32
F32R = mybir.dt.float32r
BF16 = mybir.dt.bfloat16
I32 = mybir.dt.int32
ALU = mybir.AluOpType
ACT = mybir.ActivationFunctionType


def build(nc, x, adj, w_rel1, w_root1, b1, w_rel2, w_root2, b2, a_k, out):
    x_tiles = x.rearrange("b (t p) d -> b p t d", p=P)
    adj_tiles = adj.rearrange("b (t p) n -> b p t n", p=P)
    out_tiles = out.rearrange("b (t p) d -> b p t d", p=P)

    with ExitStack() as ctx:
        def sb(name, shape, dt=F32):
            return ctx.enter_context(nc.sbuf_tensor(name, [P] + shape, dt))

        def ring(name, n, shape, dt=F32):
            return [sb(f"{name}{i}", shape, dt) for i in range(n)]

        def bank(name):
            return ctx.enter_context(nc.psum_tensor(name, [P, 512], F32))

        def sem(name):
            return ctx.enter_context(nc.semaphore(name))

        ident = sb("ident", [P])
        away_ident = sb("away_ident", [P], BF16)
        ones_bf = sb("ones_bf", [2], BF16)
        ones_r = sb("ones_r", [P], F32R)
        w_root1_sb, w_rel1_sb = sb("w_root1_sb", [DIM]), sb("w_rel1_sb", [DIM])
        w_root2_sb, w_rel2_sb = sb("w_root2_sb", [DIM]), sb("w_rel2_sb", [DIM])
        b1_col = sb("b1_col", [1])
        a_cols = sb("a_cols", [KINDS])
        minus_one = sb("minus_one", [1])
        b2_rows = sb("b2_rows", [DIM])
        b2_hi = sb("b2_hi", [DIM], F32R)
        b2_parts = sb("b2_parts", [DIM], F32R)
        minus_half = sb("minus_half", [TILES])

        x_in = ring("x_in", UNROLL, [TILES, DIM])
        adj_in = ring("adj_in", 2, [TILES, NODES], I32)
        mask = ring("mask", UNROLL, [TILES, NODES], F32R)
        unmask = ring("unmask", UNROLL, [TILES, NODES], BF16)
        stats1 = ring("stats1", 2, [TILES, 6])
        mean_var1 = ring("mean_var1", 2, [TILES, 2])
        neg_mean1 = ring("neg_mean1", 2, [TILES])
        var_eps1 = ring("var_eps1", 2, [TILES])
        rstd1 = ring("rstd1", 2, [TILES])
        z1 = ring("z1", 2, [TILES, DIM])
        h_hi = ring("h_hi", 2, [TILES, DIM], F32R)
        h_lo = ring("h_lo", 2, [TILES, DIM], F32R)
        deg = ring("deg", 2, [TILES])
        inv_deg = ring("inv_deg", 2, [TILES])
        inv_deg_bc = ring("inv_deg_bc", 2, [NODES])
        hT = sb("hT", [NODES])
        agg1T = sb("agg1T", [NODES])
        e1T = sb("e1T", [NODES])
        a1T = sb("a1T", [NODES])
        y1T = ring("y1T", 2, [NODES])
        y1_hi = sb("y1_hi", [TILES, DIM], F32R)
        y1_lo = sb("y1_lo", [TILES, DIM], F32R)
        agg2T = sb("agg2T", [NODES])
        e2 = sb("e2", [TILES, DIM])
        x_minus_1 = ring("x_minus_1", 2, [TILES, DIM])
        q2 = sb("q2", [TILES, DIM])
        x2 = ring("x2", UNROLL, [TILES, DIM])
        stats2 = ring("stats2", 2, [TILES, 6])
        mean_var2 = ring("mean_var2", 2, [TILES, 2])
        neg_mean2 = ring("neg_mean2", 2, [TILES])
        var_eps2 = ring("var_eps2", 2, [TILES])
        rstd2 = ring("rstd2", 2, [TILES])
        z2 = ring("z2", 2, [TILES, DIM])
        h3 = ring("h3", 2, [TILES, VCOLS])
        h3T = ring("h3T", 2, [NODES])
        g3T = ring("g3T", 2, [NODES])
        t4 = ring("t4", 2, [NODES])
        score = ring("score", 2, [NODES])
        row_max = ring("row_max", 2, [TILES])
        shifted = ring("shifted", 2, [NODES])
        probT = ring("probT", 2, [TILES, P])
        inv_sum = ring("inv_sum", 2, [TILES])
        y_out = ring("y_out", 2, [TILES, DIM])
        above_1 = sb("above_1", [TILES, NODES], BF16)
        above_sums = sb("above_sums", [BATCHES])
        above_sum = sb("above_sum", [1])
        other_kinds = sb("other_kinds", [1], I32)
        ones_col = sb("ones_col", [1])
        x2_kept = sb("x2_kept", [BATCHES, TILES, DIM])

        gnn_a, gnn_c, gnn_b = bank("gnn_a"), bank("gnn_c"), bank("gnn_b")
        score_ps = [bank("score_ps0"), bank("score_ps1")]
        probT_ps = [bank("probT_ps0"), bank("probT_ps1")]
        value_ps = bank("value_ps")
        kind_ps = [score_ps[0], score_ps[1], gnn_a, gnn_c]

        s_weights = sem("s_weights")
        s_x = [sem(f"s_xin{i}") for i in range(UNROLL)]
        s_adj = [sem(f"s_adjin{i}") for i in range(2)]
        s_out = [sem(f"s_out{i}") for i in range(2)]
        s_ident0, s_ident, s_away, s_const = sem("s_ident0"), sem("s_ident"), sem("s_away"), sem("s_const")
        s_b2, s_b2hi, s_b2parts = sem("s_b2"), sem("s_b2hi"), sem("s_b2parts")
        s_mask, s_unmask = sem("s_mask"), sem("s_unmask")
        s_stats1, s_mv1, s_lnin1 = sem("s_stats1"), sem("s_mv1"), sem("s_lnin1")
        s_rstd1, s_z1, s_hhi, s_hlo = sem("s_rstd1"), sem("s_z1"), sem("s_hhi"), sem("s_hlo")
        s_deg, s_degmax, s_invdeg = sem("s_deg"), sem("s_degmax"), sem("s_invdeg")
        s_bc, s_invbc = sem("s_bc"), sem("s_invbc")
        s_zT, s_hT, s_agg1, s_agg1T = sem("s_zT"), sem("s_hT"), sem("s_agg1"), sem("s_agg1T")
        s_v1, s_e1, s_a1, s_y1T = sem("s_v1"), sem("s_e1"), sem("s_a1"), sem("s_y1T")
        s_y1, s_y1hi, s_y1lo = sem("s_y1"), sem("s_y1hi"), sem("s_y1lo")
        s_agg2, s_agg2T, s_v2, s_e2 = sem("s_agg2"), sem("s_agg2T"), sem("s_v2"), sem("s_e2")
        s_xm1, s_q2, s_x2 = sem("s_xm1"), sem("s_q2"), sem("s_x2")
        s_stats2, s_mv2, s_lnin2 = sem("s_stats2"), sem("s_mv2"), sem("s_lnin2")
        s_rstd2, s_z2, s_h3, s_z2T = sem("s_rstd2"), sem("s_z2"), sem("s_h3"), sem("s_z2T")
        s_h3T, s_g3T = sem("s_h3T"), sem("s_g3T")
        s_score, s_t4, s_max, s_shift = sem("s_score"), sem("s_t4"), sem("s_max"), sem("s_shift")
        s_shiftT, s_prob, s_value = sem("s_shiftT"), sem("s_prob"), sem("s_value")
        s_invsum, s_y = sem("s_invsum"), sem("s_y")
        s_above = sem("s_above")
        s_kept = [sem(f"s_kept{i}") for i in range(UNROLL)]
        s_asum, s_atotal, s_kinds = sem("s_asum"), sem("s_atotal"), sem("s_kinds")
        r_in, r_unmask, r_out = sem("r_in"), sem("r_unmask"), sem("r_out")
        r_stats, r_mv, r_lnin, r_rstd = sem("r_stats"), sem("r_mv"), sem("r_lnin"), sem("r_rstd")
        r_z, r_h3, r_zT, r_h3T, r_g = sem("r_z"), sem("r_h3"), sem("r_zT"), sem("r_h3T"), sem("r_g")
        r_score, r_most, r_t4, r_max = sem("r_score"), sem("r_most"), sem("r_t4"), sem("r_max")
        r_shift, r_shiftT, r_prob = sem("r_shift"), sem("r_shiftT"), sem("r_prob")
        r_value, r_inv, r_y = sem("r_value"), sem("r_inv"), sem("r_y")

        def nth(b, k=1, per=1):
            loop, off = b
            return loop * (UNROLL * per) + (off * per + k)

        def arrivals(b, slots):
            loop, off = b
            return loop * (UNROLL // slots * 16) + 16 * (off // slots + 1)

        def wait_alone(eng, s_held, *waits):
            waits = [(s_done, v if isinstance(v, int) else eng.to_reg(v)) for s_done, v in waits]
            eng.wait_ge(s_held, 1)
            for s_done, v in waits:
                eng.wait_ge(s_done, v)

        def ago(b, n):
            return (b[0], b[1] - n)

        def has(b, n):
            return not isinstance(b[0], int) or b[1] >= n

        def steps(eng, step):
            for s in range(-1, 3):
                step(s, 0)
            with eng.Fori(0, 3) as loop:
                for u in range(3, 3 + UNROLL):
                    step(u, loop)
            for s in range(15, BATCHES + 2):
                step(s, 0)

        def stages(s, loop):
            found = [(loop, s + 1), (loop, s), (loop, s - 1), (loop, s - 2)]
            if isinstance(loop, int):
                found = [b if 0 <= b[1] < BATCHES else None for b in found]
            return found

        def second_pass(eng, batch):
            eng.wait_ge(s_kinds, 1)
            found = eng.value_load(other_kinds[0:1, 0:1], min_val=0, max_val=1)
            with eng.If_ne(eng.to_reg(found), 0):
                with eng.Fori(0, BATCHES) as i:
                    batch(i)

        def count(i, k=1, per=1):
            return i * per + k

        block = ctx.enter_context(nc.Block())

        @block.sync
        def _(sp):
            def load(b, first=False):
                loop, off = b
                row = loop * UNROLL + off
                if has(b, UNROLL):
                    sp.wait_ge(s_xm1, nth(ago(b, UNROLL)))
                sp.dma_start(x_in[off % UNROLL][:], x_tiles[bass.ds(row, 1), :, :, :].rearrange("b p t d -> (b p) t d")
                             ).then_inc(s_x[off % UNROLL], 16)
                if has(b, 2):
                    sp.wait_ge(s_mask, nth(ago(b, 2)))
                    sp.wait_ge(s_above, nth(ago(b, 2)))
                sp.dma_start(adj_in[off % 2][:], adj_tiles[bass.ds(row, 1), :, :, :].rearrange("b p t n -> (b p) t n")
                             ).then_inc(s_adj[off % 2], 16)

            def store(b):
                loop, off = b
                sp.wait_ge(s_x2, nth(b))
                sp.dma_start(x2_kept[:, bass.ds(loop * UNROLL + off, 1), :, :].rearrange("p b t d -> p (b t) d"),
                             x2[off % UNROLL][:]).then_inc(s_kept[off % UNROLL], 16)
                sp.wait_ge(s_y, nth(b, TILES, TILES))
                sp.dma_start(out_tiles[bass.ds(loop * UNROLL + off, 1), :, :, :].rearrange("b p t d -> (b p) t d"),
                             y_out[off % 2][:]).then_inc(s_out[off % 2], 16)

            load((0, 0))
            for dst, src in ((w_root1_sb, w_root1), (w_rel1_sb, w_rel1[RELATION]),
                             (w_root2_sb, w_root2), (w_rel2_sb, w_rel2[RELATION])):
                sp.dma_start(dst[:], src).then_inc(s_weights, 16)
            sp.dma_start(b1_col[:], b1.rearrange("(d a) -> d a", a=1)).then_inc(s_weights, 16)
            for k in range(KINDS):
                sp.dma_start(a_cols[:, k:k + 1], a_k[k]).then_inc(s_weights, 16)
            sp.wait_ge(s_const, 1)
            for part in (0, 32):
                sp.dma_start(b2_rows[part:part + 1, :], b2.rearrange("(a d) -> a d", a=1)).then_inc(s_b2, 16)

            def step(s, loop):
                ahead, _, _, att = [(loop, s + 2), None, None, (loop, s - 2)]
                if not isinstance(loop, int) or ahead[1] < BATCHES:
                    load(ahead)
                if not isinstance(loop, int) or att[1] >= 0:
                    store(att)
            for s in range(-1, 2):
                step(s, 0)
            with sp.Fori(0, 3) as loop:
                for u in range(2, 2 + UNROLL):
                    load((loop, u + 2))
                    store((loop, u - 2))
            for s in range(14, BATCHES + 2):
                step(s, 0)
            for i in range(2):
                sp.wait_ge(s_out[i], 16 * BATCHES // 2)
            for i in range(UNROLL):
                sp.wait_ge(s_kept[i], 16 * BATCHES // UNROLL)

            def batch(i):
                sp.dma_start(adj_in[0][:], adj_tiles[bass.ds(i, 1), :, :, :].rearrange("b p t n -> (b p) t n")
                             ).then_inc(r_in, 16)
                sp.dma_start(x2[0][:], x2_kept[:, bass.ds(i, 1), :, :].rearrange("p b t d -> p (b t) d")
                             ).then_inc(r_in, 16)
                sp.wait_ge(r_y, count(i, TILES, TILES))
                sp.dma_start(out_tiles[bass.ds(i, 1), :, :, :].rearrange("b p t d -> (b p) t d"),
                             y_out[0][:]).then_inc(r_out, 16)
                wait_alone(sp, s_kinds, (r_out, count(i, 16, 16)))
            second_pass(sp, batch)

        @block.gpsimd
        def _(pool):
            nc.gpsimd.memset(ident[:], 0.0).then_inc(s_ident0, 1)
            nc.gpsimd.memset(minus_half[:], -0.5)
            pool.wait_ge(s_ident0, 1)
            nc.gpsimd.affine_select(out=ident[:], in_=ident[:], compare_op=ALU.not_equal, fill=1.0, base=0,
                                    pattern=[[-1, P]], channel_multiplier=1).then_inc(s_ident, 1)

            def step(s, loop):
                load, gnn1, gnn2, att = stages(s, loop)
                if gnn2:
                    nc.gpsimd.tensor_scalar(x_minus_1[gnn2[1] % 2][:], x_in[gnn2[1] % UNROLL][:], 1.0, -1.0,
                                            ALU.mult, ALU.add).then_inc(s_xm1, 1)
                if load:
                    slot, slot2 = load[1] % UNROLL, load[1] % 2
                    pool.wait_ge(s_x[slot], arrivals(load, UNROLL))
                    pool.wait_ge(s_lnin1, nth(load))
                    nc.gpsimd.tensor_tensor(rstd1[slot2][:], var_eps1[slot2][:], minus_half[:],
                                            ALU.pow).then_inc(s_rstd1, 1)
                    z1_free = []
                    if has(load, 2):
                        z1_free = [(s_hlo, nth(ago(load, 2))), (s_zT, nth(ago(load, 2)))]
                    wait_alone(pool, s_ident, (s_rstd1, nth(load)), *z1_free)
                    for t in range(TILES):
                        last = nc.gpsimd.tensor_scalar(z1[slot2][:, t, :], x_in[slot][:, t, :],
                                                       neg_mean1[slot2][:, t:t + 1], rstd1[slot2][:, t:t + 1],
                                                       ALU.add, ALU.mult)
                    last.then_inc(s_z1, 1)
                    unmask_free = []
                    if has(load, UNROLL):
                        unmask_free = [(s_score, nth(ago(load, UNROLL), TILES, TILES))]
                    wait_alone(pool, s_ident, (s_mask, nth(load)), *unmask_free)
                    nc.gpsimd.tensor_scalar(unmask[slot][:], mask[slot][:].bitcast(F32), 1.0, -1.0,
                                            ALU.mult, ALU.add).then_inc(s_unmask, 1)
                if gnn2:
                    slot2 = gnn2[1] % 2
                    pool.wait_ge(s_lnin2, nth(gnn2))
                    nc.gpsimd.tensor_tensor(rstd2[slot2][:], var_eps2[slot2][:], minus_half[:],
                                            ALU.pow).then_inc(s_rstd2, 1)
                    wait_alone(pool, s_ident, (s_rstd2, nth(gnn2)), (s_x2, nth(gnn2)))
                    for t in range(TILES):
                        last = nc.gpsimd.tensor_scalar(z2[slot2][:, t, :], x2[gnn2[1] % UNROLL][:, t, :],
                                                       neg_mean2[slot2][:, t:t + 1], rstd2[slot2][:, t:t + 1],
                                                       ALU.add, ALU.mult)
                    last.then_inc(s_z2, 1)
            steps(pool, step)

            def batch(i):
                pool.wait_ge(r_lnin, count(i))
                nc.gpsimd.tensor_tensor(rstd2[0][:], var_eps2[0][:], minus_half[:], ALU.pow).then_inc(r_rstd, 1)
                wait_alone(pool, s_ident, (r_rstd, count(i)))
                for t in range(TILES):
                    last = nc.gpsimd.tensor_scalar(z2[0][:, t, :], x2[0][:, t, :], neg_mean2[0][:, t:t + 1],
                                                   rstd2[0][:, t:t + 1], ALU.add, ALU.mult)
                last.then_inc(r_z, 1)
            second_pass(pool, batch)

        @block.scalar
        def _(act):
            act.wait_ge(s_const, 1)

            def step(s, loop):
                load, gnn1, gnn2, att = stages(s, loop)
                if isinstance(loop, int) and s == 0:
                    act.wait_ge(s_weights, WEIGHTS * 16)

                def t4_of(t):
                    act.wait_ge(s_score, nth(att, t + 1, TILES))
                    if t >= 2 or has(att, 1):
                        act.wait_ge(s_max, nth(att, t + 1 - 2, TILES))
                    nc.scalar.activation(t4[t % 2][:], score_ps[t % 2][:], ACT.Relu,
                                         scale=(1 - SLOPE) / SLOPE).then_inc(s_t4, 1)

                def exp_of(t):
                    act.wait_ge(s_shiftT, nth(att, t + 1, TILES))
                    if t >= 2 or has(att, 1):
                        act.wait_ge(s_value, nth(att, t + 1 - 2, TILES))
                    nc.scalar.activation(probT[t % 2][:], probT_ps[t % 2][:], ACT.Exp).then_inc(s_prob, 1)

                if gnn2:
                    act.wait_ge(s_y1, nth(gnn2))
                    if has(gnn2, 1):
                        act.wait_ge(s_agg2, nth(ago(gnn2, 1)))
                    nc.scalar.activation(y1_hi[:], gnn_b[:], ACT.Copy).then_inc(s_y1hi, 1)
                if att:
                    t4_of(0)
                    t4_of(1)
                    exp_of(0)
                if gnn1:
                    act.wait_ge(s_bc, nth(gnn1))
                    if has(gnn1, 2):
                        act.wait_ge(s_agg2T, nth(ago(gnn1, 2)))
                    nc.scalar.activation(inv_deg_bc[gnn1[1] % 2][:], gnn_a[:], ACT.Copy).then_inc(s_invbc, 1)
                if gnn1:
                    act.wait_ge(s_zT, nth(gnn1))
                    if has(gnn1, 1):
                        act.wait_ge(s_v1, nth(ago(gnn1, 1)))
                    nc.scalar.activation(hT[:], gnn_c[:], ACT.Relu).then_inc(s_hT, 1)
                if gnn2:
                    act.wait_ge(s_v2, nth(gnn2))
                    if has(gnn2, 1):
                        act.wait_ge(s_q2, nth(ago(gnn2, 1)))
                    nc.scalar.activation(e2[:], gnn_b[:], ACT.Exp).then_inc(s_e2, 1)
                if att:
                    exp_of(1)
                    t4_of(2)
                if load:
                    row, off = load[0] * UNROLL + load[1], load[1]
                    act.wait_ge(s_adj[off % 2], arrivals(load, 2))
                    if has(load, 1):
                        act.wait_ge(s_above, nth(ago(load, 1)))
                    nc.scalar.activation(above_1[:], adj_in[off % 2][:], ACT.Relu, bias=minus_one[:, 0:1],
                                         accum_out=above_sums[:, bass.ds(row, 1)]
                                         ).then_inc(s_above, 1)
                if att:
                    t4_of(3)
                    exp_of(2)
                if gnn1:
                    act.wait_ge(s_v1, nth(gnn1))
                    if has(gnn1, 1):
                        act.wait_ge(s_a1, nth(ago(gnn1, 1)))
                    nc.scalar.activation(e1T[:], gnn_c[:], ACT.Exp, bias=b1_col[:, 0:1]).then_inc(s_e1, 1)
                if att:
                    exp_of(3)
                if gnn2:
                    slot2 = gnn2[1] % 2
                    act.wait_ge(s_z2T, nth(gnn2))
                    if has(gnn2, 2):
                        act.wait_ge(s_score, nth(ago(gnn2, 2), TILES, TILES))
                    nc.scalar.activation(h3T[slot2][:], gnn_b[:], ACT.Relu).then_inc(s_h3T, 1)
                    act.wait_ge(s_h3T, nth(gnn2))
                    nc.scalar.activation(g3T[slot2][:], h3T[slot2][:], ACT.Copy,
                                         scale=a_cols[:, 0:1]).then_inc(s_g3T, 1)
            steps(act, step)

            g_k = [g3T[0], g3T[1], agg1T, agg2T]

            def batch(i):
                act.wait_ge(r_zT, count(i))
                nc.scalar.activation(h3T[0][:], gnn_b[:], ACT.Relu).then_inc(r_h3T, 1)
                act.wait_ge(r_h3T, count(i))
                for k in range(KINDS):
                    nc.scalar.activation(g_k[k][:], h3T[0][:], ACT.Copy, scale=a_cols[:, k:k + 1]).then_inc(r_g, 1)
                for t in range(TILES):
                    act.wait_ge(r_most, count(i, (t + 1) * KINDS, TILES * KINDS))
                    nc.scalar.activation(t4[0][:], score[0][:], ACT.Relu,
                                         scale=(1 - SLOPE) / SLOPE).then_inc(r_t4, 1)
                    act.wait_ge(r_shiftT, count(i, t + 1, TILES))
                    nc.scalar.activation(probT[0][:], probT_ps[0][:], ACT.Exp).then_inc(r_prob, 1)
            second_pass(act, batch)

        @block.vector
        def _(dve):
            nc.vector.memset(minus_one[:], -1.0)
            nc.vector.memset(ones_col[:], 1.0)
            nc.vector.memset(b2_rows[:], 0.0).then_inc(s_const, 1)
            nc.vector.memset(ones_bf[:], 1.0)
            nc.vector.memset(h3[0][:], 1.0)
            nc.vector.memset(h3[1][:], 1.0)
            dve.wait_ge(s_ident, 1)
            nc.vector.tensor_scalar(away_ident[:], ident[:], AWAY, None, ALU.mult)
            nc.vector.tensor_scalar(ones_r[:], ident[:], 0.0, 1.0, ALU.mult, ALU.add).then_inc(s_away, 1)

            def moments(src, stats, mean_var, neg_mean, var_eps, s_stats, s_mv, s_lnin, done):
                for t in range(TILES):
                    last = nc.vector.bn_stats(stats[:, t, :], src[:, t, :])
                last.then_inc(s_stats, 1)
                wait_alone(dve, s_const, (s_stats, done))
                for t in range(TILES):
                    last = nc.vector.bn_aggr(mean_var[:, t, :], stats[:, t, :])
                last.then_inc(s_mv, 1)
                dve.wait_ge(s_mv, done)
                nc.vector.tensor_scalar(neg_mean[:], mean_var[:, :, 0], -1.0, None, ALU.mult)
                nc.vector.tensor_scalar(var_eps[:], mean_var[:, :, 1], LN_EPS, None, ALU.add).then_inc(s_lnin, 1)

            def split_b2():
                dve.wait_ge(s_b2, 32)
                dve.wait_ge(s_const, 1)
                nc.vector.tensor_scalar(b2_hi[:], b2_rows[:], 1.0, None, ALU.mult)
                nc.vector.tensor_scalar(b2_parts[:], b2_rows[:], 1.0, None, ALU.mult).then_inc(s_b2hi, 1)
                dve.wait_ge(s_b2hi, 1)
                nc.vector.tensor_tensor(b2_parts[32:64, :], b2_rows[32:64, :], b2_hi[32:64, :].bitcast(F32),
                                        ALU.subtract).then_inc(s_b2parts, 1)

            def step(s, loop):
                load, gnn1, gnn2, att = stages(s, loop)
                if isinstance(loop, int) and s == 0:
                    split_b2()
                    dve.wait_ge(s_weights, WEIGHTS * 16)

                def max_of(t):
                    wait_alone(dve, s_const, (s_t4, nth(att, t + 1, TILES)))
                    nc.vector.tensor_tensor_reduce(
                        out=score[t % 2][:], in0=score_ps[t % 2][:], in1=t4[t % 2][:], scale=SLOPE,
                        scalar=-3e38, op0=ALU.add, op1=ALU.max,
                        accum_out=row_max[att[1] % 2][:, t:t + 1]).then_inc(s_max, 1)
                    dve.wait_ge(s_max, nth(att, t + 1, TILES))
                    if t >= 2 or has(att, 1):
                        dve.wait_ge(s_shiftT, nth(att, t + 1 - 2, TILES))
                    nc.vector.tensor_scalar(shifted[t % 2][:], score[t % 2][:], row_max[att[1] % 2][:, t:t + 1],
                                            None, ALU.subtract).then_inc(s_shift, 1)

                def out_of(t):
                    slot2 = att[1] % 2
                    if t == 0 and has(att, 2):
                        dve.wait_ge(s_out[slot2], arrivals(ago(att, 2), 2))
                    dve.wait_ge(s_value, nth(att, t + 1, TILES))
                    nc.vector.reciprocal(inv_sum[slot2][:, t:t + 1], value_ps[:, DIM:DIM + 1]).then_inc(s_invsum, 1)
                    dve.wait_ge(s_invsum, nth(att, t + 1, TILES))
                    nc.vector.scalar_tensor_tensor(out=y_out[slot2][:, t, :], in0=value_ps[:, 0:DIM],
                                                   scalar=inv_sum[slot2][:, t:t + 1],
                                                   in1=x2[att[1] % UNROLL][:, t, :],
                                                   op0=ALU.mult, op1=ALU.add).then_inc(s_y, 1)

                if gnn2:
                    dve.wait_ge(s_y1hi, nth(gnn2))
                    if has(gnn2, 1):
                        dve.wait_ge(s_agg2, nth(ago(gnn2, 1)))
                    nc.vector.tensor_tensor(y1_lo[:], gnn_b[:], y1_hi[:].bitcast(F32),
                                            ALU.subtract).then_inc(s_y1lo, 1)
                if att:
                    max_of(0)
                if gnn1:
                    slot2 = gnn1[1] % 2
                    dve.wait_ge(s_deg, nth(gnn1))
                    nc.vector.tensor_scalar(deg[slot2][:], gnn_a[:, 0:2 * TILES:2], float(NODES), 1.0,
                                            ALU.add, ALU.max).then_inc(s_degmax, 1)
                    dve.wait_ge(s_degmax, nth(gnn1))
                    nc.vector.reciprocal(inv_deg[slot2][:], deg[slot2][:]).then_inc(s_invdeg, 1)
                if att:
                    max_of(1)
                if gnn2:
                    dve.wait_ge(s_agg2, nth(gnn2))
                    dve.wait_ge(s_invbc, nth(gnn2))
                    nc.vector.tensor_tensor(agg2T[:], gnn_b[:], inv_deg_bc[gnn2[1] % 2][:],
                                            ALU.mult).then_inc(s_agg2T, 1)
                if load:
                    slot, slot2 = load[1] % UNROLL, load[1] % 2
                    dve.wait_ge(s_x[slot], arrivals(load, UNROLL))
                    if has(load, 2):
                        dve.wait_ge(s_z1, nth(ago(load, 2)))
                    moments(x_in[slot], stats1[slot2], mean_var1[slot2], neg_mean1[slot2], var_eps1[slot2],
                            s_stats1, s_mv1, s_lnin1, nth(load))
                if load:
                    slot, slot2 = load[1] % UNROLL, load[1] % 2
                    dve.wait_ge(s_adj[slot2], arrivals(load, 2))
                    if has(load, UNROLL):
                        dve.wait_ge(s_agg2, nth(ago(load, UNROLL)))
                        dve.wait_ge(s_unmask, nth(ago(load, UNROLL)))
                    nc.vector.tensor_scalar(mask[slot][:], adj_in[slot2][:], 1.0, None,
                                            ALU.is_equal).then_inc(s_mask, 1)
                if gnn2:
                    slot2 = gnn2[1] % 2
                    dve.wait_ge(s_e2, nth(gnn2))
                    dve.wait_ge(s_xm1, nth(gnn2))
                    nc.vector.scalar_tensor_tensor(out=q2[:], in0=e2[:], scalar=1.0, in1=x_minus_1[slot2][:],
                                                   op0=ALU.min, op1=ALU.add).then_inc(s_q2, 1)
                    dve.wait_ge(s_q2, nth(gnn2))
                    if has(gnn2, UNROLL):
                        dve.wait_ge(s_kept[gnn2[1] % UNROLL], arrivals(ago(gnn2, UNROLL), UNROLL))
                    nc.vector.scalar_tensor_tensor(out=x2[gnn2[1] % UNROLL][:], in0=gnn_b[:].rearrange("p (t d) -> p t d", t=TILES),
                                                   scalar=0.0, in1=q2[:], op0=ALU.max, op1=ALU.add).then_inc(s_x2, 1)
                if att:
                    out_of(0)
                if gnn2:
                    slot2 = gnn2[1] % 2
                    dve.wait_ge(s_x2, nth(gnn2))
                    moments(x2[gnn2[1] % UNROLL], stats2[slot2], mean_var2[slot2], neg_mean2[slot2],
                            var_eps2[slot2], s_stats2, s_mv2, s_lnin2, nth(gnn2))
                if att:
                    max_of(2)
                if gnn1:
                    dve.wait_ge(s_agg1, nth(gnn1))
                    dve.wait_ge(s_invbc, nth(gnn1))
                    nc.vector.tensor_tensor(agg1T[:], gnn_a[:], inv_deg_bc[gnn1[1] % 2][:],
                                            ALU.mult).then_inc(s_agg1T, 1)
                if att:
                    out_of(1)
                    max_of(3)
                if load:
                    slot2 = load[1] % 2
                    dve.wait_ge(s_z1, nth(load))
                    if has(load, 2):
                        dve.wait_ge(s_agg1, nth(ago(load, 2)))
                    nc.vector.tensor_scalar(h_hi[slot2][:], z1[slot2][:], 0.0, None, ALU.max).then_inc(s_hhi, 1)
                    dve.wait_ge(s_hhi, nth(load))
                    nc.vector.scalar_tensor_tensor(out=h_lo[slot2][:], in0=z1[slot2][:], scalar=0.0,
                                                   in1=h_hi[slot2][:].bitcast(F32), op0=ALU.max,
                                                   op1=ALU.subtract).then_inc(s_hlo, 1)
                if gnn2:
                    dve.wait_ge(s_z2, nth(gnn2))
                    if has(gnn2, 2):
                        dve.wait_ge(s_value, nth(ago(gnn2, 2), TILES, TILES))
                    nc.vector.tensor_scalar(h3[gnn2[1] % 2][:, :, 0:DIM], z2[gnn2[1] % 2][:], 0.0, None,
                                            ALU.max).then_inc(s_h3, 1)
                if att:
                    out_of(2)
                if gnn1:
                    slot2 = gnn1[1] % 2
                    dve.wait_ge(s_e1, nth(gnn1))
                    nc.vector.tensor_scalar(a1T[:], e1T[:], 1.0, -1.0, ALU.min, ALU.add).then_inc(s_a1, 1)
                    dve.wait_ge(s_a1, nth(gnn1))
                    if has(gnn1, 2):
                        dve.wait_ge(s_v2, nth(ago(gnn1, 2)))
                    nc.vector.scalar_tensor_tensor(out=y1T[slot2][:], in0=gnn_c[:], scalar=b1_col[:, 0:1],
                                                   in1=a1T[:], op0=ALU.add, op1=ALU.max).then_inc(s_y1T, 1)
                if att:
                    out_of(3)
                if isinstance(loop, int) and s == BATCHES:
                    dve.wait_ge(s_above, BATCHES)
                    nc.vector.reduce_max(above_sum[:], above_sums[:], mybir.AxisListType.X).then_inc(s_asum, 1)
            steps(dve, step)
            dve.wait_ge(s_atotal, 1)
            nc.vector.tensor_scalar(other_kinds[0:1, :], gnn_a[0:1, 0:1], 1.0, None, ALU.min).then_inc(s_kinds, 1)

            def batch(i):
                dve.wait_ge(r_in, count(i, 32, 32))
                for k in range(KINDS):
                    nc.vector.tensor_scalar(unmask[k][:], adj_in[0][:], float(k + 1), -1.0,
                                            ALU.is_equal, ALU.add).then_inc(r_unmask, 1)
                moments(x2[0], stats2[0], mean_var2[0], neg_mean2[0], var_eps2[0], r_stats, r_mv, r_lnin, count(i))
                dve.wait_ge(r_z, count(i))
                nc.vector.tensor_scalar(h3[0][:, :, 0:DIM], z2[0][:], 0.0, None, ALU.max).then_inc(r_h3, 1)
                for t in range(TILES):
                    dve.wait_ge(r_score, count(i, t + 1, TILES))
                    nc.vector.tensor_copy(score[0][:], kind_ps[0][:]).then_inc(r_most, 1)
                    for k in range(1, KINDS):
                        dve.wait_ge(r_most, count(i, t * KINDS + k, TILES * KINDS))
                        nc.vector.tensor_tensor(score[0][:], kind_ps[k][:], score[0][:], ALU.max).then_inc(r_most, 1)
                    wait_alone(dve, s_const, (r_t4, count(i, t + 1, TILES)))
                    nc.vector.tensor_tensor_reduce(
                        out=score[1][:], in0=score[0][:], in1=t4[0][:], scale=SLOPE, scalar=-3e38,
                        op0=ALU.add, op1=ALU.max, accum_out=row_max[0][:, t:t + 1]).then_inc(r_max, 1)
                    dve.wait_ge(r_max, count(i, t + 1, TILES))
                    nc.vector.tensor_scalar(shifted[0][:], score[1][:], row_max[0][:, t:t + 1], None,
                                            ALU.subtract).then_inc(r_shift, 1)
                    dve.wait_ge(r_value, count(i, t + 1, TILES))
                    nc.vector.reciprocal(inv_sum[0][:, t:t + 1], value_ps[:, DIM:DIM + 1]).then_inc(r_inv, 1)
                    dve.wait_ge(r_inv, count(i, t + 1, TILES))
                    nc.vector.scalar_tensor_tensor(out=y_out[0][:, t, :], in0=value_ps[:, 0:DIM],
                                                   scalar=inv_sum[0][:, t:t + 1], in1=x2[0][:, t, :],
                                                   op0=ALU.mult, op1=ALU.add).then_inc(r_y, 1)
            second_pass(dve, batch)

        @block.tensor
        def _(pe):
            pe.wait_ge(s_away, 1)
            pe.wait_ge(s_ident, 1)

            def tiled(t):
                return slice(t * P, (t + 1) * P)

            def step(s, loop):
                load, gnn1, gnn2, att = stages(s, loop)
                if isinstance(loop, int) and s == 0:
                    pe.wait_ge(s_b2parts, 1)
                    pe.wait_ge(s_weights, WEIGHTS * 16)

                def score_of(t):
                    slot, slot2 = att[1] % UNROLL, att[1] % 2
                    if t == 0:
                        pe.wait_ge(s_unmask, nth(att))
                        pe.wait_ge(s_g3T, nth(att))
                    if t >= 2 or has(att, 1):
                        pe.wait_ge(s_max, nth(att, t + 1 - 2, TILES))
                    nc.tensor.matmul(score_ps[t % 2][:], away_ident[:], unmask[slot][:, t, :],
                                     start=True, stop=False)
                    nc.tensor.matmul(score_ps[t % 2][:], g3T[slot2][:, tiled(t)], h3T[slot2][:],
                                     start=False, stop=True).then_inc(s_score, 1)

                def shiftT_of(t):
                    pe.wait_ge(s_shift, nth(att, t + 1, TILES))
                    if t >= 2 or has(att, 1):
                        pe.wait_ge(s_prob, nth(att, t + 1 - 2, TILES))
                    for j in range(TILES):
                        last = nc.tensor.transpose(probT_ps[t % 2][:, tiled(j)], shifted[t % 2][:, tiled(j)], ident[:])
                    last.then_inc(s_shiftT, 1)

                def value_of(t):
                    pe.wait_ge(s_prob, nth(att, t + 1, TILES))
                    if t == 0:
                        pe.wait_ge(s_h3, nth(att))
                    if t >= 1 or has(att, 1):
                        pe.wait_ge(s_y, nth(att, t + 1 - 1, TILES))
                    for j in range(TILES):
                        last = nc.tensor.matmul(value_ps[:, 0:VCOLS], probT[t % 2][:, j, :],
                                                h3[att[1] % 2][:, j, :], start=(j == 0), stop=(j == TILES - 1))
                    last.then_inc(s_value, 1)

                def aggregate(ps, parts, masks, s_done):
                    steps_left = [(part, t) for part in parts for t in range(TILES)]
                    for n, (part, t) in enumerate(steps_left):
                        last = nc.tensor.matmul(ps[:], part[:, t, :], masks[:, t, :], start=(n == 0),
                                                stop=(n == len(steps_left) - 1))
                    last.then_inc(s_done, 1)

                if gnn2:
                    pe.wait_ge(s_y1T, nth(gnn2))
                    if has(gnn2, 1):
                        pe.wait_ge(s_h3T, nth(ago(gnn2, 1)))
                    for t in range(TILES):
                        last = nc.tensor.transpose(gnn_b[:, tiled(t)], y1T[gnn2[1] % 2][:, tiled(t)], ident[:])
                    last.then_inc(s_y1, 1)
                if att:
                    score_of(0)
                if att:
                    score_of(1)
                if gnn2:
                    pe.wait_ge(s_y1hi, nth(gnn2))
                    pe.wait_ge(s_y1lo, nth(gnn2))
                    aggregate(gnn_b, (y1_hi, y1_lo), mask[gnn2[1] % UNROLL], s_agg2)
                if att:
                    shiftT_of(0)
                if gnn1:
                    pe.wait_ge(s_invdeg, nth(gnn1))
                    for t in range(TILES):
                        last = nc.tensor.transpose(gnn_a[:, tiled(t)],
                                                   inv_deg[gnn1[1] % 2][:, t:t + 1].broadcast_to([P, P]), ident[:])
                    last.then_inc(s_bc, 1)
                if gnn1:
                    pe.wait_ge(s_z1, nth(gnn1))
                    if has(gnn1, 1):
                        pe.wait_ge(s_y1T, nth(ago(gnn1, 1)))
                    for t in range(TILES):
                        last = nc.tensor.transpose(gnn_c[:, tiled(t)], z1[gnn1[1] % 2][:, t, :], ident[:])
                    last.then_inc(s_zT, 1)
                if gnn2:
                    pe.wait_ge(s_agg2T, nth(gnn2))
                    nc.tensor.matmul(gnn_b[:], ones_r[:], b2_parts[:].rearrange("p (a d) -> p a d", a=1)
                                     .broadcast_to([P, TILES, DIM]), start=True, stop=False)
                    for t in range(TILES):
                        nc.tensor.matmul(gnn_b[:, tiled(t)], y1T[gnn2[1] % 2][:, tiled(t)], w_root2_sb[:],
                                         start=False, stop=False)
                        last = nc.tensor.matmul(gnn_b[:, tiled(t)], agg2T[:, tiled(t)], w_rel2_sb[:],
                                                start=False, stop=(t == TILES - 1))
                    last.then_inc(s_v2, 1)
                if att:
                    shiftT_of(1)
                    value_of(0)
                    score_of(2)
                if gnn1:
                    pe.wait_ge(s_invbc, nth(gnn1))
                    pe.wait_ge(s_hlo, nth(gnn1))
                    aggregate(gnn_a, (h_hi[gnn1[1] % 2], h_lo[gnn1[1] % 2]), mask[gnn1[1] % UNROLL], s_agg1)
                if att:
                    value_of(1)
                    score_of(3)
                    shiftT_of(2)
                if gnn1:
                    pe.wait_ge(s_hT, nth(gnn1))
                    nc.tensor.matmul(gnn_c[:], w_root1_sb[:], hT[:], start=True, stop=False)
                    pe.wait_ge(s_agg1T, nth(gnn1))
                    nc.tensor.matmul(gnn_c[:], w_rel1_sb[:], agg1T[:], start=False, stop=True).then_inc(s_v1, 1)
                if att:
                    value_of(2)
                    shiftT_of(3)
                if gnn2:
                    pe.wait_ge(s_z2, nth(gnn2))
                    pe.wait_ge(s_x2, nth(gnn2))
                    for t in range(TILES):
                        last = nc.tensor.transpose(gnn_b[:, tiled(t)], z2[gnn2[1] % 2][:, t, :], ident[:])
                    last.then_inc(s_z2T, 1)
                if load:
                    slot = load[1] % UNROLL
                    pe.wait_ge(s_unmask, nth(load))
                    if has(load, 1):
                        pe.wait_ge(s_agg1T, nth(ago(load, 1)))
                    for j in range(TILES):
                        for t in range(TILES):
                            last = nc.tensor.matmul(gnn_a[:, 2 * j:2 * j + 2], unmask[slot][:, t, tiled(j)],
                                                    ones_bf[:], start=(t == 0), stop=(t == TILES - 1))
                    last.then_inc(s_deg, 1)
                if att:
                    value_of(3)
                if isinstance(loop, int) and s == BATCHES + 1:
                    pe.wait_ge(s_asum, 1)
                    pe.wait_ge(s_agg1T, BATCHES)
                    nc.tensor.matmul(gnn_a[0:1, 0:1], above_sum[:], ones_col[:], start=True,
                                     stop=True).then_inc(s_atotal, 1)
            steps(pe, step)

            g_k = [g3T[0], g3T[1], agg1T, agg2T]

            def batch(i):
                pe.wait_ge(r_z, count(i))
                for t in range(TILES):
                    last = nc.tensor.transpose(gnn_b[:, tiled(t)], z2[0][:, t, :], ident[:])
                last.then_inc(r_zT, 1)
                pe.wait_ge(r_unmask, count(i, KINDS, KINDS))
                pe.wait_ge(r_g, count(i, KINDS, KINDS))
                pe.wait_ge(r_h3, count(i))
                for t in range(TILES):
                    if t > 0:
                        pe.wait_ge(r_most, count(i, t * KINDS, TILES * KINDS))
                    for k in range(KINDS):
                        nc.tensor.matmul(kind_ps[k][:], away_ident[:], unmask[k][:, t, :], start=True, stop=False)
                        last = nc.tensor.matmul(kind_ps[k][:], g_k[k][:, tiled(t)], h3T[0][:],
                                                start=False, stop=True)
                    last.then_inc(r_score, 1)
                    pe.wait_ge(r_shift, count(i, t + 1, TILES))
                    for j in range(TILES):
                        last = nc.tensor.transpose(probT_ps[0][:, tiled(j)], shifted[0][:, tiled(j)], ident[:])
                    last.then_inc(r_shiftT, 1)
                    pe.wait_ge(r_prob, count(i, t + 1, TILES))
                    if t > 0:
                        pe.wait_ge(r_y, count(i, t, TILES))
                    for j in range(TILES):
                        last = nc.tensor.matmul(value_ps[:, 0:VCOLS], probT[0][:, j, :], h3[0][:, j, :],
                                                start=(j == 0), stop=(j == TILES - 1))
                    last.then_inc(r_value, 1)
            second_pass(pe, batch)


_INS = ['x', 'adj', 'L0_gnn_w_rel1', 'L0_gnn_w_root1', 'L0_gnn_b1', 'L0_gnn_w_rel2', 'L0_gnn_w_root2',
        'L0_gnn_b2']
_KINDS = ['L1_gnn_a_0', 'L1_gnn_a_1', 'L1_gnn_a_2', 'L1_gnn_a_3']


def kernel(**inputs):
    import numpy as _np
    import concourse.bacc as _bacc
    from concourse import mybir as _mybir
    from concourse.bass_utils import run_bass_kernel_spmd as _run

    nc = _bacc.Bacc("TRN2", target_bir_lowering=False, num_devices=1)
    arrays, args = {}, []
    for name in _INS + _KINDS:
        a = _np.ascontiguousarray(inputs[name])
        arrays[f"in_{name}"] = a
        args.append(nc.dram_tensor(f"in_{name}", a.shape, _mybir.dt.from_np(a.dtype), kind="ExternalInput").ap())
    out = nc.dram_tensor("out", (BATCHES, NODES, DIM), F32, kind="ExternalOutput").ap()
    build(nc, *args[:len(_INS)], args[len(_INS):], out)
    r = _run(nc, [arrays], core_ids=[0])
    return r.results[0]["out"]
```

```python
from contextlib import ExitStack

import concourse.bass as bass
from concourse import mybir

P = 128
BATCHES, NODES, DIM = 16, 512, 128
TILES = NODES // P
RELATION = 1
LN_EPS = 1e-5
SLOPE = 0.2
NEG_INF = -9e15
AWAY = -NEG_INF / SLOPE
KINDS = 4
ACT_SHIFTS = (1,)
UNROLL = 4
WARM_UPS = 20, 6, 4
WEIGHTS = 5 + KINDS
VCOLS = DIM + 2

F32 = mybir.dt.float32
F32R = mybir.dt.float32r
BF16 = mybir.dt.bfloat16
I32 = mybir.dt.int32
ALU = mybir.AluOpType
ACT = mybir.ActivationFunctionType


def build(nc, x, adj, w_rel1, w_root1, b1, w_rel2, w_root2, b2, a_k, out):
    x_tiles = x.rearrange("b (t p) d -> b p t d", p=P)
    adj_tiles = adj.rearrange("b (t p) n -> b p t n", p=P)
    out_tiles = out.rearrange("b (t p) d -> b p t d", p=P)

    with ExitStack() as ctx:
        def sb(name, shape, dt=F32):
            return ctx.enter_context(nc.sbuf_tensor(name, [P] + shape, dt))

        def ring(name, n, shape, dt=F32):
            return [sb(f"{name}{i}", shape, dt) for i in range(n)]

        def bank(name):
            return ctx.enter_context(nc.psum_tensor(name, [P, 512], F32))

        def sem(name):
            return ctx.enter_context(nc.semaphore(name))

        ident = sb("ident", [P])
        away_ident = sb("away_ident", [P], BF16)
        ones_bf = sb("ones_bf", [2], BF16)
        ones_r = sb("ones_r", [P], F32R)
        w_root1_sb, w_rel1_sb = sb("w_root1_sb", [DIM]), sb("w_rel1_sb", [DIM])
        w_root2_sb, w_rel2_sb = sb("w_root2_sb", [DIM]), sb("w_rel2_sb", [DIM])
        b1_col = sb("b1_col", [1])
        a_cols = sb("a_cols", [KINDS])
        minus_one = sb("minus_one", [1])
        b2_rows = sb("b2_rows", [DIM])
        b2_hi = sb("b2_hi", [DIM], F32R)
        b2_parts = sb("b2_parts", [DIM], F32R)
        minus_half = sb("minus_half", [TILES])

        x_in = ring("x_in", UNROLL, [TILES, DIM])
        adj_in = ring("adj_in", 2, [TILES, NODES], I32)
        mask = ring("mask", UNROLL, [TILES, NODES], F32R)
        unmask = ring("unmask", UNROLL, [TILES, NODES], BF16)
        stats1 = ring("stats1", 2, [TILES, 6])
        mean_var1 = ring("mean_var1", 2, [TILES, 2])
        neg_mean1 = ring("neg_mean1", 2, [TILES])
        var_eps1 = ring("var_eps1", 2, [TILES])
        rstd1 = ring("rstd1", 2, [TILES])
        z1 = ring("z1", 2, [TILES, DIM])
        h_hi = ring("h_hi", 2, [TILES, DIM], F32R)
        h_lo = ring("h_lo", 2, [TILES, DIM], F32R)
        deg = ring("deg", 2, [TILES])
        inv_deg = ring("inv_deg", 2, [TILES])
        inv_deg_bc = ring("inv_deg_bc", 2, [NODES])
        hT = sb("hT", [NODES])
        agg1T = sb("agg1T", [NODES])
        e1T = sb("e1T", [NODES])
        a1T = sb("a1T", [NODES])
        y1T = ring("y1T", 2, [NODES])
        y1_hi = sb("y1_hi", [TILES, DIM], F32R)
        y1_lo = sb("y1_lo", [TILES, DIM], F32R)
        agg2T = sb("agg2T", [NODES])
        e2 = sb("e2", [TILES, DIM])
        x_minus_1 = ring("x_minus_1", 2, [TILES, DIM])
        q2 = sb("q2", [TILES, DIM])
        x2 = ring("x2", UNROLL, [TILES, DIM])
        stats2 = ring("stats2", 2, [TILES, 6])
        mean_var2 = ring("mean_var2", 2, [TILES, 2])
        neg_mean2 = ring("neg_mean2", 2, [TILES])
        var_eps2 = ring("var_eps2", 2, [TILES])
        rstd2 = ring("rstd2", 2, [TILES])
        z2 = sb("z2", [TILES, DIM])
        h3 = ring("h3", 2, [TILES, VCOLS])
        h3T_hi = ring("h3T_hi", 2, [NODES], F32R)
        h3T_lo = ring("h3T_lo", 2, [NODES], F32R)
        g3T_hi = ring("g3T_hi", 2, [NODES], F32R)
        g3T_lo = ring("g3T_lo", 2, [NODES], F32R)
        t4 = ring("t4", 2, [NODES])
        score = ring("score", 2, [NODES])
        row_max = ring("row_max", 2, [TILES])
        shifted = ring("shifted", 2, [NODES])
        probT = ring("probT", 2, [TILES, P])
        inv_sum = ring("inv_sum", 2, [TILES])
        y_out = ring("y_out", 2, [TILES, DIM])
        above_1 = sb("above_1", [TILES, NODES], BF16)
        above_sums = sb("above_sums", [2 * BATCHES])
        above_sum = sb("above_sum", [1])
        other_kinds = sb("other_kinds", [1], I32)
        ones_col = sb("ones_col", [1])
        x2_kept = sb("x2_kept", [BATCHES, TILES, DIM])

        gnn_a, gnn_c, gnn_b = bank("gnn_a"), bank("gnn_c"), bank("gnn_b")
        score_ps = [bank("score_ps0"), bank("score_ps1")]
        probT_ps = [bank("probT_ps0"), bank("probT_ps1")]
        value_ps = bank("value_ps")
        kind_ps = [score_ps[0], score_ps[1], gnn_a, gnn_c]

        s_weights = sem("s_weights")
        s_x = [sem(f"s_xin{i}") for i in range(UNROLL)]
        s_adj = [sem(f"s_adjin{i}") for i in range(2)]
        s_out = [sem(f"s_out{i}") for i in range(2)]
        s_ident0, s_ident, s_away = sem("s_ident0"), sem("s_ident"), sem("s_away")
        s_ones, s_const = sem("s_ones"), sem("s_const")
        s_b2, s_b2hi, s_b2parts = sem("s_b2"), sem("s_b2hi"), sem("s_b2parts")
        s_mask, s_unmask = sem("s_mask"), sem("s_unmask")
        s_stats1, s_mv1, s_lnin1 = sem("s_stats1"), sem("s_mv1"), sem("s_lnin1")
        s_rstd1, s_z1, s_hhi, s_hlo = sem("s_rstd1"), sem("s_z1"), sem("s_hhi"), sem("s_hlo")
        s_deg, s_degmax, s_invdeg = sem("s_deg"), sem("s_degmax"), sem("s_invdeg")
        s_bc, s_invbc = sem("s_bc"), sem("s_invbc")
        s_zT, s_hT, s_agg1, s_agg1T = sem("s_zT"), sem("s_hT"), sem("s_agg1"), sem("s_agg1T")
        s_v1, s_e1, s_a1, s_y1T = sem("s_v1"), sem("s_e1"), sem("s_a1"), sem("s_y1T")
        s_y1, s_y1hi, s_y1lo = sem("s_y1"), sem("s_y1hi"), sem("s_y1lo")
        s_agg2, s_agg2T, s_v2, s_e2 = sem("s_agg2"), sem("s_agg2T"), sem("s_v2"), sem("s_e2")
        s_xm1, s_q2, s_x2 = sem("s_xm1"), sem("s_q2"), sem("s_x2")
        s_stats2, s_mv2, s_lnin2 = sem("s_stats2"), sem("s_mv2"), sem("s_lnin2")
        s_rstd2, s_z2, s_h3, s_h3T = sem("s_rstd2"), sem("s_z2"), sem("s_h3"), sem("s_h3T")
        s_h3Thi, s_h3Tlo = sem("s_h3Thi"), sem("s_h3Tlo")
        s_g3Thi, s_g3Tlo = sem("s_g3Thi"), sem("s_g3Tlo")
        s_score, s_t4, s_max, s_shift = sem("s_score"), sem("s_t4"), sem("s_max"), [sem("s_shift0"), sem("s_shift1")]
        s_shiftT, s_prob, s_value = sem("s_shiftT"), sem("s_prob"), sem("s_value")
        s_invsum, s_y = sem("s_invsum"), sem("s_y")
        s_above = [sem("s_above0"), sem("s_above1")]
        s_kept = [sem(f"s_kept{i}") for i in range(UNROLL)]
        s_asum, s_atotal, s_kinds = sem("s_asum"), sem("s_atotal"), sem("s_kinds")
        r_in, r_unmask, r_out = sem("r_in"), sem("r_unmask"), sem("r_out")
        r_stats, r_mv, r_lnin, r_rstd = sem("r_stats"), sem("r_mv"), sem("r_lnin"), sem("r_rstd")
        r_z, r_h3, r_zT, r_h3T, r_g = sem("r_z"), sem("r_h3"), sem("r_zT"), sem("r_h3T"), sem("r_g")
        r_score, r_most, r_t4, r_max = sem("r_score"), sem("r_most"), sem("r_t4"), sem("r_max")
        r_shift, r_shiftT, r_prob = sem("r_shift"), sem("r_shiftT"), sem("r_prob")
        r_value, r_inv, r_y = sem("r_value"), sem("r_inv"), sem("r_y")

        def nth(b, k=1, per=1):
            loop, off = b
            return loop * (UNROLL * per) + (off * per + k)

        def arrivals(b, slots):
            loop, off = b
            return loop * (UNROLL // slots * 16) + 16 * (off // slots + 1)

        def wait_alone(eng, s_held, *waits):
            waits = [(s_done, v if isinstance(v, int) else eng.to_reg(v)) for s_done, v in waits]
            eng.wait_ge(s_held, 1)
            for s_done, v in waits:
                eng.wait_ge(s_done, v)

        def ago(b, n):
            return (b[0], b[1] - n)

        def has(b, n):
            return not isinstance(b[0], int) or b[1] >= n

        def steps(eng, step):
            for s in range(-1, 3):
                step(s, 0)
            with eng.Fori(0, 3) as loop:
                for u in range(3, 3 + UNROLL):
                    step(u, loop)
            for s in range(15, BATCHES + 2):
                step(s, 0)

        def stages(s, loop):
            found = [(loop, s + 1), (loop, s), (loop, s - 1), (loop, s - 2)]
            if isinstance(loop, int):
                found = [b if 0 <= b[1] < BATCHES else None for b in found]
            return found

        def value_bank(t, gnn1):
            return gnn_c if t % 2 and not gnn1 else value_ps

        def second_pass(eng, batch):
            eng.wait_ge(s_kinds, 1)
            found = eng.value_load(other_kinds[0:1, 0:1], min_val=0, max_val=1)
            with eng.If_ne(eng.to_reg(found), 0):
                with eng.Fori(0, BATCHES) as i:
                    batch(i)

        def count(i, k=1, per=1):
            return i * per + k

        block = ctx.enter_context(nc.Block())

        @block.sync
        def _(sp):
            def load(b, first=False):
                loop, off = b
                row = loop * UNROLL + off
                if has(b, UNROLL):
                    sp.wait_ge(s_xm1, nth(ago(b, UNROLL)))
                sp.dma_start(x_in[off % UNROLL][:], x_tiles[bass.ds(row, 1), :, :, :].rearrange("b p t d -> (b p) t d")
                             ).then_inc(s_x[off % UNROLL], 16)
                if has(b, 2):
                    sp.wait_ge(s_mask, nth(ago(b, 2)))
                    for half in range(2):
                        sp.wait_ge(s_above[half], nth(ago(b, 2)))
                sp.dma_start(adj_in[off % 2][:], adj_tiles[bass.ds(row, 1), :, :, :].rearrange("b p t n -> (b p) t n")
                             ).then_inc(s_adj[off % 2], 16)

            def store(b):
                loop, off = b
                sp.wait_ge(s_x2, nth(b))
                sp.dma_start(x2_kept[:, bass.ds(loop * UNROLL + off, 1), :, :].rearrange("p b t d -> p (b t) d"),
                             x2[off % UNROLL][:]).then_inc(s_kept[off % UNROLL], 16)
                sp.wait_ge(s_y, nth(b, TILES, TILES))
                sp.dma_start(out_tiles[bass.ds(loop * UNROLL + off, 1), :, :, :].rearrange("b p t d -> (b p) t d"),
                             y_out[off % 2][:]).then_inc(s_out[off % 2], 16)

            load((0, 0))
            for dst, src in ((w_root1_sb, w_root1), (w_rel1_sb, w_rel1[RELATION]),
                             (w_root2_sb, w_root2), (w_rel2_sb, w_rel2[RELATION])):
                sp.dma_start(dst[:], src).then_inc(s_weights, 16)
            sp.dma_start(b1_col[:], b1.rearrange("(d a) -> d a", a=1)).then_inc(s_weights, 16)
            for k in range(KINDS):
                sp.dma_start(a_cols[:, k:k + 1], a_k[k]).then_inc(s_weights, 16)
            load((0, 1))
            sp.wait_ge(s_const, 1)
            for part in (0, 32):
                sp.dma_start(b2_rows[part:part + 1, :], b2.rearrange("(a d) -> a d", a=1)).then_inc(s_b2, 16)

            def step(s, loop):
                ahead, _, _, att = [(loop, s + 2), None, None, (loop, s - 2)]
                if not isinstance(loop, int) or ahead[1] < BATCHES:
                    load(ahead)
                if not isinstance(loop, int) or att[1] >= 0:
                    store(att)
            for s in range(0, 2):
                step(s, 0)
            with sp.Fori(0, 3) as loop:
                for u in range(2, 2 + UNROLL):
                    load((loop, u + 2))
                    store((loop, u - 2))
            for s in range(14, BATCHES + 2):
                step(s, 0)
            for i in range(2):
                sp.wait_ge(s_out[i], 16 * BATCHES // 2)
            for i in range(UNROLL):
                sp.wait_ge(s_kept[i], 16 * BATCHES // UNROLL)

            def batch(i):
                sp.dma_start(adj_in[0][:], adj_tiles[bass.ds(i, 1), :, :, :].rearrange("b p t n -> (b p) t n")
                             ).then_inc(r_in, 16)
                sp.dma_start(x2[0][:], x2_kept[:, bass.ds(i, 1), :, :].rearrange("p b t d -> p (b t) d")
                             ).then_inc(r_in, 16)
                sp.wait_ge(r_y, count(i, TILES, TILES))
                sp.dma_start(out_tiles[bass.ds(i, 1), :, :, :].rearrange("b p t d -> (b p) t d"),
                             y_out[0][:]).then_inc(r_out, 16)
                wait_alone(sp, s_kinds, (r_out, count(i, 16, 16)))
            second_pass(sp, batch)

        @block.gpsimd
        def _(pool):
            nc.gpsimd.memset(ident[:], 0.0).then_inc(s_ident0, 1)
            nc.gpsimd.memset(minus_half[:], -0.5)
            pool.wait_ge(s_ident0, 1)
            nc.gpsimd.affine_select(out=ident[:], in_=ident[:], compare_op=ALU.not_equal, fill=1.0, base=0,
                                    pattern=[[-1, P]], channel_multiplier=1).then_inc(s_ident, 1)

            def step(s, loop):
                load, gnn1, gnn2, att = stages(s, loop)

                def z1_of():
                    slot, slot2 = load[1] % UNROLL, load[1] % 2
                    z1_free = []
                    if has(load, 2):
                        z1_free = [(s_hlo, nth(ago(load, 2))), (s_zT, nth(ago(load, 2)))]
                    wait_alone(pool, s_ident, (s_rstd1, nth(load)), *z1_free)
                    for t in range(TILES):
                        last = nc.gpsimd.tensor_scalar(z1[slot2][:, t, :], x_in[slot][:, t, :],
                                                       neg_mean1[slot2][:, t:t + 1], rstd1[slot2][:, t:t + 1],
                                                       ALU.add, ALU.mult)
                    last.then_inc(s_z1, 1)

                if gnn2:
                    nc.gpsimd.tensor_scalar(x_minus_1[gnn2[1] % 2][:], x_in[gnn2[1] % UNROLL][:], 1.0, -1.0,
                                            ALU.mult, ALU.add).then_inc(s_xm1, 1)
                if load:
                    slot, slot2 = load[1] % UNROLL, load[1] % 2
                    pool.wait_ge(s_x[slot], arrivals(load, UNROLL))
                    pool.wait_ge(s_lnin1, nth(load))
                    nc.gpsimd.tensor_tensor(rstd1[slot2][:], var_eps1[slot2][:], minus_half[:],
                                            ALU.pow).then_inc(s_rstd1, 1)
                    if not gnn2:
                        z1_of()
                    if gnn1:
                        unmask_free = []
                        if has(load, UNROLL):
                            unmask_free = [(s_score, nth(ago(load, UNROLL), TILES, TILES))]
                        wait_alone(pool, s_ident, (s_mask, nth(load)), *unmask_free)
                        nc.gpsimd.tensor_scalar(unmask[slot][:], mask[slot][:].bitcast(F32), 1.0, -1.0,
                                                ALU.mult, ALU.add).then_inc(s_unmask, 1)
                if gnn2:
                    slot2 = gnn2[1] % 2
                    pool.wait_ge(s_lnin2, nth(gnn2))
                    nc.gpsimd.tensor_tensor(rstd2[slot2][:], var_eps2[slot2][:], minus_half[:],
                                            ALU.pow).then_inc(s_rstd2, 1)
                    z2_free = [(s_h3, nth(ago(gnn2, 1)))] if has(gnn2, 1) else []
                    wait_alone(pool, s_ident, (s_rstd2, nth(gnn2)), (s_x2, nth(gnn2)), *z2_free)
                    for t in range(TILES):
                        last = nc.gpsimd.tensor_scalar(z2[:, t, :], x2[gnn2[1] % UNROLL][:, t, :],
                                                       neg_mean2[slot2][:, t:t + 1], rstd2[slot2][:, t:t + 1],
                                                       ALU.add, ALU.mult)
                    last.then_inc(s_z2, 1)
                    if load:
                        z1_of()
            steps(pool, step)

            def batch(i):
                pool.wait_ge(r_lnin, count(i))
                nc.gpsimd.tensor_tensor(rstd2[0][:], var_eps2[0][:], minus_half[:], ALU.pow).then_inc(r_rstd, 1)
                wait_alone(pool, s_ident, (r_rstd, count(i)))
                for t in range(TILES):
                    last = nc.gpsimd.tensor_scalar(z2[:, t, :], x2[0][:, t, :], neg_mean2[0][:, t:t + 1],
                                                   rstd2[0][:, t:t + 1], ALU.add, ALU.mult)
                last.then_inc(r_z, 1)
            second_pass(pool, batch)

        @block.scalar
        def _(act):
            act.wait_ge(s_ident, 1)
            nc.scalar.activation(away_ident[:], ident[:], ACT.Copy, scale=AWAY).then_inc(s_away, 1)
            act.wait_ge(s_const, 1)

            def step(s, loop):
                load, gnn1, gnn2, att = stages(s, loop)

                def t4_of(t):
                    act.wait_ge(s_score, nth(att, t + 1, TILES))
                    if t >= 2 or has(att, 1):
                        act.wait_ge(s_max, nth(att, t + 1 - 2, TILES))
                    nc.scalar.activation(t4[t % 2][:], score_ps[t % 2][:], ACT.Relu,
                                         scale=(1 - SLOPE) / SLOPE).then_inc(s_t4, 1)

                def exp_of(t):
                    act.wait_ge(s_shiftT, nth(att, t + 1, TILES))
                    if t >= 2 or has(att, 1):
                        act.wait_ge(s_value, nth(att, t + 1 - 2, TILES))
                    nc.scalar.activation(probT[t % 2][:], probT_ps[t % 2][:], ACT.Exp,
                                         scale=-1.0 if t in ACT_SHIFTS else 1.0).then_inc(s_prob, 1)

                def look_at(half):
                    slot2, tiles = gnn1[1] % 2, slice(half * TILES // 2, (half + 1) * TILES // 2)
                    act.wait_ge(s_adj[slot2], arrivals(gnn1, 2))
                    if has(gnn1, 1):
                        act.wait_ge(s_above[half], nth(ago(gnn1, 1)))
                    nc.scalar.activation(above_1[:, tiles, :], adj_in[slot2][:, tiles, :], ACT.Relu,
                                         bias=minus_one[:, 0:1],
                                         accum_out=above_sums[:, bass.ds(gnn1[0] * (2 * UNROLL) + 2 * gnn1[1] + half, 1)]
                                         ).then_inc(s_above[half], 1)

                def shift_of(t):
                    act.wait_ge(s_max, nth(att, t + 1, TILES))
                    if t >= 2 or has(att, 1):
                        act.wait_ge(s_shiftT, nth(att, t + 1 - 2, TILES))
                    nc.scalar.activation(shifted[t % 2][:], score[t % 2][:], ACT.Identity, scale=-1.0,
                                         bias=row_max[att[1] % 2][:, t:t + 1]).then_inc(s_shift[t % 2], 1)

                if gnn2:
                    act.wait_ge(s_y1, nth(gnn2))
                    if has(gnn2, 1):
                        act.wait_ge(s_agg2, nth(ago(gnn2, 1)))
                    nc.scalar.activation(y1_hi[:], gnn_b[:], ACT.Copy).then_inc(s_y1hi, 1)
                if att:
                    t4_of(0)
                if gnn1:
                    act.wait_ge(s_zT, nth(gnn1))
                    if has(gnn1, 1):
                        act.wait_ge(s_v1, nth(ago(gnn1, 1)))
                    nc.scalar.activation(hT[:], gnn_c[:], ACT.Relu).then_inc(s_hT, 1)
                if att:
                    t4_of(1)
                if gnn1:
                    act.wait_ge(s_z1, nth(gnn1))
                    if has(gnn1, 2):
                        act.wait_ge(s_agg1, nth(ago(gnn1, 2)))
                    nc.scalar.activation(h_hi[gnn1[1] % 2][:], z1[gnn1[1] % 2][:], ACT.Relu).then_inc(s_hhi, 1)
                if att:
                    t4_of(2)
                if gnn2:
                    act.wait_ge(s_v2, nth(gnn2))
                    if has(gnn2, 1):
                        act.wait_ge(s_q2, nth(ago(gnn2, 1)))
                    nc.scalar.activation(e2[:], gnn_b[:], ACT.Exp).then_inc(s_e2, 1)
                if gnn1 and att:
                    look_at(1)
                if gnn1:
                    act.wait_ge(s_bc, nth(gnn1))
                    if has(gnn1, 2):
                        act.wait_ge(s_agg2T, nth(ago(gnn1, 2)))
                    nc.scalar.activation(inv_deg_bc[gnn1[1] % 2][:], gnn_a[:], ACT.Copy).then_inc(s_invbc, 1)
                if gnn1 and not att:
                    look_at(0)
                    look_at(1)
                if gnn1 and att:
                    look_at(0)
                if att:
                    exp_of(0)
                    shift_of(1)
                    t4_of(3)
                    exp_of(1)
                if gnn1:
                    if not has(gnn1, 1):
                        act.wait_ge(s_weights, WEIGHTS * 16)
                    act.wait_ge(s_v1, nth(gnn1))
                    if has(gnn1, 1):
                        act.wait_ge(s_a1, nth(ago(gnn1, 1)))
                    nc.scalar.activation(e1T[:], gnn_c[:], ACT.Exp, bias=b1_col[:, 0:1]).then_inc(s_e1, 1)
                if att:
                    exp_of(2)
                    exp_of(3)
                if gnn2:
                    slot2 = gnn2[1] % 2
                    act.wait_ge(s_h3T, nth(gnn2))
                    if has(gnn2, 2):
                        act.wait_ge(s_score, nth(ago(gnn2, 2), TILES, TILES))
                    nc.scalar.activation(h3T_hi[slot2][:], gnn_a[:], ACT.Copy).then_inc(s_h3Thi, 1)
                    nc.scalar.activation(g3T_hi[slot2][:], gnn_a[:], ACT.Copy,
                                         scale=a_cols[:, 0:1]).then_inc(s_g3Thi, 1)
            steps(act, step)

            h3T, g_k = hT, [a1T, e1T, agg1T, agg2T]

            def batch(i):
                act.wait_ge(r_zT, count(i))
                nc.scalar.activation(h3T[:], gnn_b[:], ACT.Relu).then_inc(r_h3T, 1)
                act.wait_ge(r_h3T, count(i))
                for k in range(KINDS):
                    nc.scalar.activation(g_k[k][:], h3T[:], ACT.Copy, scale=a_cols[:, k:k + 1]).then_inc(r_g, 1)
                for t in range(TILES):
                    act.wait_ge(r_most, count(i, (t + 1) * KINDS, TILES * KINDS))
                    nc.scalar.activation(t4[0][:], score[0][:], ACT.Relu,
                                         scale=(1 - SLOPE) / SLOPE).then_inc(r_t4, 1)
                    act.wait_ge(r_shiftT, count(i, t + 1, TILES))
                    nc.scalar.activation(probT[0][:], probT_ps[0][:], ACT.Exp).then_inc(r_prob, 1)
            second_pass(act, batch)

        @block.vector
        def _(dve):
            nc.vector.memset(minus_one[:], -1.0)
            nc.vector.memset(ones_col[:], 1.0)
            nc.vector.memset(b2_rows[:], 0.0).then_inc(s_const, 1)
            nc.vector.memset(ones_bf[:], 1.0)
            nc.vector.memset(h3[0][:], 1.0)
            nc.vector.memset(h3[1][:], 1.0)
            dve.wait_ge(s_ident, 1)
            nc.vector.tensor_scalar(ones_r[:], ident[:], 0.0, 1.0, ALU.mult, ALU.add).then_inc(s_ones, 1)

            def moments(src, stats, mean_var, neg_mean, var_eps, s_stats, s_mv, s_lnin, done):
                for t in range(TILES):
                    last = nc.vector.bn_stats(stats[:, t, :], src[:, t, :])
                last.then_inc(s_stats, 1)
                wait_alone(dve, s_const, (s_stats, done))
                for t in range(TILES):
                    last = nc.vector.bn_aggr(mean_var[:, t, :], stats[:, t, :])
                last.then_inc(s_mv, 1)
                dve.wait_ge(s_mv, done)
                nc.vector.tensor_scalar(neg_mean[:], mean_var[:, :, 0], -1.0, None, ALU.mult)
                nc.vector.tensor_scalar(var_eps[:], mean_var[:, :, 1], LN_EPS, None, ALU.add).then_inc(s_lnin, 1)

            def split_b2():
                dve.wait_ge(s_b2, 32)
                dve.wait_ge(s_const, 1)
                nc.vector.tensor_scalar(b2_hi[:], b2_rows[:], 1.0, None, ALU.mult)
                nc.vector.tensor_scalar(b2_parts[:], b2_rows[:], 1.0, None, ALU.mult).then_inc(s_b2hi, 1)
                dve.wait_ge(s_b2hi, 1)
                nc.vector.tensor_tensor(b2_parts[32:64, :], b2_rows[32:64, :], b2_hi[32:64, :].bitcast(F32),
                                        ALU.subtract).then_inc(s_b2parts, 1)

            def step(s, loop):
                load, gnn1, gnn2, att = stages(s, loop)
                if isinstance(loop, int) and s == 1:
                    split_b2()

                def max_of(t):
                    score_free = []
                    if t >= 2 or has(att, 1):
                        score_free = [(s_shift[t % 2], nth(att, t // 2 + 1 - 1, TILES // 2))]
                    wait_alone(dve, s_const, (s_t4, nth(att, t + 1, TILES)), *score_free)
                    nc.vector.tensor_tensor_reduce(
                        out=score[t % 2][:], in0=score_ps[t % 2][:], in1=t4[t % 2][:], scale=SLOPE,
                        scalar=-3e38, op0=ALU.add, op1=ALU.max,
                        accum_out=row_max[att[1] % 2][:, t:t + 1]).then_inc(s_max, 1)

                def mask_of():
                    slot, slot2 = load[1] % UNROLL, load[1] % 2
                    dve.wait_ge(s_adj[slot2], arrivals(load, 2))
                    if has(load, UNROLL):
                        dve.wait_ge(s_agg2, nth(ago(load, UNROLL)))
                        dve.wait_ge(s_unmask, nth(ago(load, UNROLL)))
                    nc.vector.tensor_scalar(mask[slot][:], adj_in[slot2][:], 1.0, None,
                                            ALU.is_equal).then_inc(s_mask, 1)
                    if not gnn1:
                        dve.wait_ge(s_mask, nth(load))
                        nc.vector.tensor_scalar(unmask[slot][:], mask[slot][:].bitcast(F32), 1.0, -1.0,
                                                ALU.mult, ALU.add).then_inc(s_unmask, 1)

                def moments1():
                    slot, slot2 = load[1] % UNROLL, load[1] % 2
                    dve.wait_ge(s_x[slot], arrivals(load, UNROLL))
                    if has(load, 2):
                        dve.wait_ge(s_z1, nth(ago(load, 2)))
                    moments(x_in[slot], stats1[slot2], mean_var1[slot2], neg_mean1[slot2], var_eps1[slot2],
                            s_stats1, s_mv1, s_lnin1, nth(load))

                def shift_of(t):
                    dve.wait_ge(s_max, nth(att, t + 1, TILES))
                    if t >= 2 or has(att, 1):
                        dve.wait_ge(s_shiftT, nth(att, t + 1 - 2, TILES))
                    nc.vector.tensor_scalar(shifted[t % 2][:], score[t % 2][:], row_max[att[1] % 2][:, t:t + 1],
                                            None, ALU.subtract).then_inc(s_shift[t % 2], 1)

                def out_of(t):
                    slot2 = att[1] % 2
                    if t == 0 and has(att, 2):
                        dve.wait_ge(s_out[slot2], arrivals(ago(att, 2), 2))
                    dve.wait_ge(s_value, nth(att, t + 1, TILES))
                    values = value_bank(t, gnn1)
                    nc.vector.reciprocal(inv_sum[slot2][:, t:t + 1], values[:, DIM:DIM + 1]).then_inc(s_invsum, 1)
                    dve.wait_ge(s_invsum, nth(att, t + 1, TILES))
                    nc.vector.scalar_tensor_tensor(out=y_out[slot2][:, t, :], in0=values[:, 0:DIM],
                                                   scalar=inv_sum[slot2][:, t:t + 1],
                                                   in1=x2[att[1] % UNROLL][:, t, :],
                                                   op0=ALU.mult, op1=ALU.add).then_inc(s_y, 1)

                if gnn2:
                    dve.wait_ge(s_y1hi, nth(gnn2))
                    if has(gnn2, 1):
                        dve.wait_ge(s_agg2, nth(ago(gnn2, 1)))
                    nc.vector.tensor_tensor(y1_lo[:], gnn_b[:], y1_hi[:].bitcast(F32),
                                            ALU.subtract).then_inc(s_y1lo, 1)
                if load and has(load, UNROLL):
                    mask_of()
                if att:
                    max_of(0)
                    max_of(1)
                if gnn2:
                    dve.wait_ge(s_agg2, nth(gnn2))
                    dve.wait_ge(s_invbc, nth(gnn2))
                    nc.vector.tensor_tensor(agg2T[:], gnn_b[:], inv_deg_bc[gnn2[1] % 2][:],
                                            ALU.mult).then_inc(s_agg2T, 1)
                if gnn1:
                    slot2 = gnn1[1] % 2
                    dve.wait_ge(s_deg, nth(gnn1))
                    nc.vector.tensor_scalar(deg[slot2][:], gnn_a[:, 0:2 * TILES:2], float(NODES), 1.0,
                                            ALU.add, ALU.max).then_inc(s_degmax, 1)
                    dve.wait_ge(s_degmax, nth(gnn1))
                    nc.vector.reciprocal(inv_deg[slot2][:], deg[slot2][:]).then_inc(s_invdeg, 1)
                if att:
                    shift_of(0)
                if gnn1:
                    slot2 = gnn1[1] % 2
                    dve.wait_ge(s_hhi, nth(gnn1))
                    if has(gnn1, 2):
                        dve.wait_ge(s_agg1, nth(ago(gnn1, 2)))
                    nc.vector.scalar_tensor_tensor(out=h_lo[slot2][:], in0=z1[slot2][:], scalar=0.0,
                                                   in1=h_hi[slot2][:].bitcast(F32), op0=ALU.max,
                                                   op1=ALU.subtract).then_inc(s_hlo, 1)
                if load:
                    moments1()
                if load and not has(load, UNROLL):
                    mask_of()
                if gnn2:
                    slot2 = gnn2[1] % 2
                    dve.wait_ge(s_e2, nth(gnn2))
                    dve.wait_ge(s_xm1, nth(gnn2))
                    nc.vector.scalar_tensor_tensor(out=q2[:], in0=e2[:], scalar=1.0, in1=x_minus_1[slot2][:],
                                                   op0=ALU.min, op1=ALU.add).then_inc(s_q2, 1)
                    dve.wait_ge(s_q2, nth(gnn2))
                    if has(gnn2, UNROLL):
                        dve.wait_ge(s_kept[gnn2[1] % UNROLL], arrivals(ago(gnn2, UNROLL), UNROLL))
                    nc.vector.scalar_tensor_tensor(out=x2[gnn2[1] % UNROLL][:], in0=gnn_b[:].rearrange("p (t d) -> p t d", t=TILES),
                                                   scalar=0.0, in1=q2[:], op0=ALU.max, op1=ALU.add).then_inc(s_x2, 1)
                if gnn2:
                    slot2 = gnn2[1] % 2
                    dve.wait_ge(s_x2, nth(gnn2))
                    moments(x2[gnn2[1] % UNROLL], stats2[slot2], mean_var2[slot2], neg_mean2[slot2],
                            var_eps2[slot2], s_stats2, s_mv2, s_lnin2, nth(gnn2))
                if att:
                    max_of(2)
                if gnn1:
                    dve.wait_ge(s_agg1, nth(gnn1))
                    dve.wait_ge(s_invbc, nth(gnn1))
                    nc.vector.tensor_tensor(agg1T[:], gnn_a[:], inv_deg_bc[gnn1[1] % 2][:],
                                            ALU.mult).then_inc(s_agg1T, 1)
                if att:
                    shift_of(2)
                    out_of(0)
                    max_of(3)
                    shift_of(3)
                if gnn2:
                    dve.wait_ge(s_z2, nth(gnn2))
                    if has(gnn2, 2):
                        dve.wait_ge(s_value, nth(ago(gnn2, 2), TILES, TILES))
                    nc.vector.tensor_scalar(h3[gnn2[1] % 2][:, :, 0:DIM], z2[:], 0.0, None,
                                            ALU.max).then_inc(s_h3, 1)
                if gnn1:
                    if not has(gnn1, 1):
                        dve.wait_ge(s_weights, WEIGHTS * 16)
                    dve.wait_ge(s_e1, nth(gnn1))
                    nc.vector.tensor_scalar(a1T[:], e1T[:], 1.0, -1.0, ALU.min, ALU.add).then_inc(s_a1, 1)
                if att:
                    out_of(1)
                if gnn1:
                    slot2 = gnn1[1] % 2
                    dve.wait_ge(s_a1, nth(gnn1))
                    if has(gnn1, 2):
                        dve.wait_ge(s_v2, nth(ago(gnn1, 2)))
                    nc.vector.scalar_tensor_tensor(out=y1T[slot2][:], in0=gnn_c[:], scalar=b1_col[:, 0:1],
                                                   in1=a1T[:], op0=ALU.add, op1=ALU.max).then_inc(s_y1T, 1)
                if att:
                    out_of(2)
                if gnn2:
                    slot2 = gnn2[1] % 2
                    dve.wait_ge(s_h3Thi, nth(gnn2))
                    dve.wait_ge(s_g3Thi, nth(gnn2))
                    if has(gnn2, 2):
                        dve.wait_ge(s_score, nth(ago(gnn2, 2), TILES, TILES))
                    nc.vector.tensor_tensor(h3T_lo[slot2][:], gnn_a[:], h3T_hi[slot2][:].bitcast(F32),
                                            ALU.subtract).then_inc(s_h3Tlo, 1)
                    nc.vector.scalar_tensor_tensor(out=g3T_lo[slot2][:], in0=gnn_a[:], scalar=a_cols[:, 0:1],
                                                   in1=g3T_hi[slot2][:].bitcast(F32), op0=ALU.mult,
                                                   op1=ALU.subtract).then_inc(s_g3Tlo, 1)
                if att:
                    out_of(3)
                if isinstance(loop, int) and s == BATCHES:
                    for half in range(2):
                        dve.wait_ge(s_above[half], BATCHES)
                    nc.vector.reduce_max(above_sum[:], above_sums[:], mybir.AxisListType.X).then_inc(s_asum, 1)
            steps(dve, step)
            dve.wait_ge(s_atotal, 1)
            nc.vector.tensor_scalar(other_kinds[0:1, :], gnn_a[0:1, 0:1], 1.0, None, ALU.min).then_inc(s_kinds, 1)

            def batch(i):
                dve.wait_ge(r_in, count(i, 32, 32))
                for k in range(KINDS):
                    nc.vector.tensor_scalar(unmask[k][:], adj_in[0][:], float(k + 1), -1.0,
                                            ALU.is_equal, ALU.add).then_inc(r_unmask, 1)
                moments(x2[0], stats2[0], mean_var2[0], neg_mean2[0], var_eps2[0], r_stats, r_mv, r_lnin, count(i))
                dve.wait_ge(r_z, count(i))
                nc.vector.tensor_scalar(h3[0][:, :, 0:DIM], z2[:], 0.0, None, ALU.max).then_inc(r_h3, 1)
                for t in range(TILES):
                    dve.wait_ge(r_score, count(i, t + 1, TILES))
                    nc.vector.tensor_copy(score[0][:], kind_ps[0][:]).then_inc(r_most, 1)
                    for k in range(1, KINDS):
                        dve.wait_ge(r_most, count(i, t * KINDS + k, TILES * KINDS))
                        nc.vector.tensor_tensor(score[0][:], kind_ps[k][:], score[0][:], ALU.max).then_inc(r_most, 1)
                    wait_alone(dve, s_const, (r_t4, count(i, t + 1, TILES)))
                    nc.vector.tensor_tensor_reduce(
                        out=score[1][:], in0=score[0][:], in1=t4[0][:], scale=SLOPE, scalar=-3e38,
                        op0=ALU.add, op1=ALU.max, accum_out=row_max[0][:, t:t + 1]).then_inc(r_max, 1)
                    dve.wait_ge(r_max, count(i, t + 1, TILES))
                    nc.vector.tensor_scalar(shifted[0][:], score[1][:], row_max[0][:, t:t + 1], None,
                                            ALU.subtract).then_inc(r_shift, 1)
                    dve.wait_ge(r_value, count(i, t + 1, TILES))
                    nc.vector.reciprocal(inv_sum[0][:, t:t + 1], value_ps[:, DIM:DIM + 1]).then_inc(r_inv, 1)
                    dve.wait_ge(r_inv, count(i, t + 1, TILES))
                    nc.vector.scalar_tensor_tensor(out=y_out[0][:, t, :], in0=value_ps[:, 0:DIM],
                                                   scalar=inv_sum[0][:, t:t + 1], in1=x2[0][:, t, :],
                                                   op0=ALU.mult, op1=ALU.add).then_inc(r_y, 1)
            second_pass(dve, batch)

        @block.tensor
        def _(pe):
            pe.wait_ge(s_ident, 1)

            def keep_warm(products):
                for _ in range(products):
                    nc.tensor.matmul(value_ps[:, 0:P], ident[:], ident[:], start=True, stop=True)

            keep_warm(WARM_UPS[0])
            pe.wait_ge(s_away, 1)
            pe.wait_ge(s_ones, 1)

            def tiled(t):
                return slice(t * P, (t + 1) * P)

            def step(s, loop):
                load, gnn1, gnn2, att = stages(s, loop)
                if isinstance(loop, int) and s == 1:
                    pe.wait_ge(s_b2parts, 1)

                def score_of(t):
                    slot, slot2 = att[1] % UNROLL, att[1] % 2
                    if t >= 2 or has(att, 1):
                        pe.wait_ge(s_max, nth(att, t + 1 - 2, TILES))
                    nc.tensor.matmul(score_ps[t % 2][:], away_ident[:], unmask[slot][:, t, :],
                                     start=True, stop=False)
                    if t == 0:
                        pe.wait_ge(s_h3Tlo, nth(att))
                        pe.wait_ge(s_g3Thi, nth(att))
                    nc.tensor.matmul(score_ps[t % 2][:], g3T_hi[slot2][:, tiled(t)], h3T_hi[slot2][:],
                                     start=False, stop=False)
                    nc.tensor.matmul(score_ps[t % 2][:], g3T_hi[slot2][:, tiled(t)], h3T_lo[slot2][:],
                                     start=False, stop=False)
                    if t == 0:
                        pe.wait_ge(s_g3Tlo, nth(att))
                    nc.tensor.matmul(score_ps[t % 2][:], g3T_lo[slot2][:, tiled(t)], h3T_hi[slot2][:],
                                     start=False, stop=True).then_inc(s_score, 1)

                def shiftT_of(t):
                    pe.wait_ge(s_shift[t % 2], nth(att, t // 2 + 1, TILES // 2))
                    if t >= 2 or has(att, 1):
                        pe.wait_ge(s_prob, nth(att, t + 1 - 2, TILES))
                    for j in range(TILES):
                        last = nc.tensor.transpose(probT_ps[t % 2][:, tiled(j)], shifted[t % 2][:, tiled(j)], ident[:])
                    last.then_inc(s_shiftT, 1)

                def value_of(t):
                    pe.wait_ge(s_prob, nth(att, t + 1, TILES))
                    if t == 0:
                        pe.wait_ge(s_h3, nth(att))
                    if t >= 1 or has(att, 1):
                        pe.wait_ge(s_y, nth(att, t if gnn1 else max(t - 1, 0), TILES))
                    for j in range(TILES):
                        last = nc.tensor.matmul(value_bank(t, gnn1)[:, 0:VCOLS], probT[t % 2][:, j, :],
                                                h3[att[1] % 2][:, j, :], start=(j == 0), stop=(j == TILES - 1))
                    last.then_inc(s_value, 1)

                def aggregate(ps, parts, masks, s_done):
                    steps_left = [(part, t) for part in parts for t in range(TILES)]
                    for n, (part, t) in enumerate(steps_left):
                        last = nc.tensor.matmul(ps[:], part[:, t, :], masks[:, t, :], start=(n == 0),
                                                stop=(n == len(steps_left) - 1))
                    last.then_inc(s_done, 1)

                if att:
                    score_of(0)
                    score_of(1)
                if gnn2:
                    if not att:
                        keep_warm(WARM_UPS[2])
                    pe.wait_ge(s_y1hi, nth(gnn2))
                    pe.wait_ge(s_y1lo, nth(gnn2))
                    aggregate(gnn_b, (y1_hi, y1_lo), mask[gnn2[1] % UNROLL], s_agg2)
                if gnn1:
                    slot = gnn1[1] % UNROLL
                    pe.wait_ge(s_unmask, nth(gnn1))
                    if has(gnn1, 2):
                        pe.wait_ge(s_g3Tlo, nth(ago(gnn1, 2)))
                    elif has(gnn1, 1):
                        pe.wait_ge(s_agg1T, nth(ago(gnn1, 1)))
                    for j in range(TILES):
                        for t in range(TILES):
                            last = nc.tensor.matmul(gnn_a[:, 2 * j:2 * j + 2], unmask[slot][:, t, tiled(j)],
                                                    ones_bf[:], start=(t == 0), stop=(t == TILES - 1))
                    last.then_inc(s_deg, 1)
                if att:
                    score_of(2)
                if gnn2:
                    pe.wait_ge(s_agg2T, nth(gnn2))
                    nc.tensor.matmul(gnn_b[:], ones_r[:], b2_parts[:].rearrange("p (a d) -> p a d", a=1)
                                     .broadcast_to([P, TILES, DIM]), start=True, stop=False)
                    for t in range(TILES):
                        nc.tensor.matmul(gnn_b[:, tiled(t)], y1T[gnn2[1] % 2][:, tiled(t)], w_root2_sb[:],
                                         start=False, stop=False)
                        last = nc.tensor.matmul(gnn_b[:, tiled(t)], agg2T[:, tiled(t)], w_rel2_sb[:],
                                                start=False, stop=(t == TILES - 1))
                    last.then_inc(s_v2, 1)
                if gnn1:
                    if not has(gnn1, 1):
                        pe.wait_ge(s_weights, WEIGHTS * 16)
                    pe.wait_ge(s_hT, nth(gnn1))
                    nc.tensor.matmul(gnn_c[:], w_root1_sb[:], hT[:], start=True, stop=False)
                if gnn1:
                    pe.wait_ge(s_invdeg, nth(gnn1))
                    for t in range(TILES):
                        last = nc.tensor.transpose(gnn_a[:, tiled(t)],
                                                   inv_deg[gnn1[1] % 2][:, t:t + 1].broadcast_to([P, P]), ident[:])
                    last.then_inc(s_bc, 1)
                if att:
                    score_of(3)
                    shiftT_of(0)
                if gnn1:
                    pe.wait_ge(s_invbc, nth(gnn1))
                    pe.wait_ge(s_hlo, nth(gnn1))
                    aggregate(gnn_a, (h_hi[gnn1[1] % 2], h_lo[gnn1[1] % 2]), mask[gnn1[1] % UNROLL], s_agg1)
                if att:
                    value_of(0)
                    shiftT_of(1)
                if gnn1:
                    pe.wait_ge(s_agg1T, nth(gnn1))
                    nc.tensor.matmul(gnn_c[:], w_rel1_sb[:], agg1T[:], start=False, stop=True).then_inc(s_v1, 1)
                if att:
                    shiftT_of(2)
                    value_of(1)
                    shiftT_of(3)
                if gnn2:
                    if not att:
                        keep_warm(WARM_UPS[2])
                    pe.wait_ge(s_h3, nth(gnn2))
                    if gnn1:
                        pe.wait_ge(s_agg1T, nth(gnn1))
                    for t in range(TILES):
                        last = nc.tensor.transpose(gnn_a[:, tiled(t)], h3[gnn2[1] % 2][:, t, 0:DIM], ident[:])
                    last.then_inc(s_h3T, 1)
                if att:
                    value_of(2)
                if load:
                    if gnn1 and not gnn2:
                        keep_warm(WARM_UPS[1])
                    pe.wait_ge(s_z1, nth(load))
                    if has(load, 1):
                        pe.wait_ge(s_y1T, nth(ago(load, 1)))
                    for t in range(TILES):
                        last = nc.tensor.transpose(gnn_c[:, tiled(t)], z1[load[1] % 2][:, t, :], ident[:])
                    last.then_inc(s_zT, 1)
                if gnn1:
                    pe.wait_ge(s_y1T, nth(gnn1))
                    if has(gnn1, 1):
                        pe.wait_ge(s_x2, nth(ago(gnn1, 1)))
                    for t in range(TILES):
                        last = nc.tensor.transpose(gnn_b[:, tiled(t)], y1T[gnn1[1] % 2][:, tiled(t)], ident[:])
                    last.then_inc(s_y1, 1)
                if att:
                    value_of(3)
                if isinstance(loop, int) and s == BATCHES + 1:
                    pe.wait_ge(s_asum, 1)
                    pe.wait_ge(s_g3Tlo, BATCHES)
                    nc.tensor.matmul(gnn_a[0:1, 0:1], above_sum[:], ones_col[:], start=True,
                                     stop=True).then_inc(s_atotal, 1)
            steps(pe, step)

            h3T, g_k = hT, [a1T, e1T, agg1T, agg2T]

            def batch(i):
                pe.wait_ge(r_z, count(i))
                for t in range(TILES):
                    last = nc.tensor.transpose(gnn_b[:, tiled(t)], z2[:, t, :], ident[:])
                last.then_inc(r_zT, 1)
                pe.wait_ge(r_unmask, count(i, KINDS, KINDS))
                pe.wait_ge(r_g, count(i, KINDS, KINDS))
                pe.wait_ge(r_h3, count(i))
                for t in range(TILES):
                    if t > 0:
                        pe.wait_ge(r_most, count(i, t * KINDS, TILES * KINDS))
                    for k in range(KINDS):
                        nc.tensor.matmul(kind_ps[k][:], away_ident[:], unmask[k][:, t, :], start=True, stop=False)
                        last = nc.tensor.matmul(kind_ps[k][:], g_k[k][:, tiled(t)], h3T[:],
                                                start=False, stop=True)
                    last.then_inc(r_score, 1)
                    pe.wait_ge(r_shift, count(i, t + 1, TILES))
                    for j in range(TILES):
                        last = nc.tensor.transpose(probT_ps[0][:, tiled(j)], shifted[0][:, tiled(j)], ident[:])
                    last.then_inc(r_shiftT, 1)
                    pe.wait_ge(r_prob, count(i, t + 1, TILES))
                    if t > 0:
                        pe.wait_ge(r_y, count(i, t, TILES))
                    for j in range(TILES):
                        last = nc.tensor.matmul(value_ps[:, 0:VCOLS], probT[0][:, j, :], h3[0][:, j, :],
                                                start=(j == 0), stop=(j == TILES - 1))
                    last.then_inc(r_value, 1)
            second_pass(pe, batch)


_INS = ['x', 'adj', 'L0_gnn_w_rel1', 'L0_gnn_w_root1', 'L0_gnn_b1', 'L0_gnn_w_rel2', 'L0_gnn_w_root2',
        'L0_gnn_b2']
_KINDS = ['L1_gnn_a_0', 'L1_gnn_a_1', 'L1_gnn_a_2', 'L1_gnn_a_3']


def kernel(**inputs):
    import numpy as _np
    import concourse.bacc as _bacc
    from concourse import mybir as _mybir
    from concourse.bass_utils import run_bass_kernel_spmd as _run

    nc = _bacc.Bacc("TRN2", target_bir_lowering=False, num_devices=1)
    arrays, args = {}, []
    for name in _INS + _KINDS:
        a = _np.ascontiguousarray(inputs[name])
        arrays[f"in_{name}"] = a
        args.append(nc.dram_tensor(f"in_{name}", a.shape, _mybir.dt.from_np(a.dtype), kind="ExternalInput").ap())
    out = nc.dram_tensor("out", (BATCHES, NODES, DIM), F32, kind="ExternalOutput").ap()
    build(nc, *args[:len(_INS)], args[len(_INS):], out)
    r = _run(nc, [arrays], core_ids=[0])
    return r.results[0]["out"]
```
